# Optimizing a Trainium2 kernel written in Bass

```python
import numpy as np
import jax
import jax.numpy as jnp

def _softmax(x, axis=-1):
    return jax.nn.softmax(x, axis=axis)

def _gelu(x):
    return jax.nn.gelu(x, approximate=True)

def _silu(x):
    return jax.nn.silu(x)

def _sigmoid(x):
    return jax.nn.sigmoid(x)

def _layernorm(x, axis=-1, eps=1e-05):
    m = jnp.mean(x, axis=axis, keepdims=True)
    v = jnp.var(x, axis=axis, keepdims=True)
    return (x - m) / jnp.sqrt(v + eps)

def _scatter_add(tgt, idx, src, axis=0):
    return tgt.at[idx].add(src)

def _segment_sum(src, seg, n):
    return jax.ops.segment_sum(src, seg, n)
kernel_name = 'mk_xattn_seq_d2_seqx_r4_308638'

def setup_inputs(seed: int=0):
    np.random.seed(seed)
    _w = jnp.asarray

    def _rec_inputs():
        import jax
        import jax.numpy as jnp
        _rk = jax.random.key(seed)
        x = 7.22e-05 + 1 * jax.random.normal(jax.random.fold_in(_rk, 1), (32, 256, 256), jnp.float32)
        _lenS = 256 - jax.random.randint(jax.random.fold_in(_rk, 7), (32,), 0, max(1, 256 // 4) + 1, jnp.int32)
        _lenS2 = 256 - jax.random.randint(jax.random.fold_in(_rk, 8), (32,), 0, max(1, 256 // 4) + 1, jnp.int32)
        _ctx_1024P = jax.random.normal(jax.random.fold_in(_rk, 11), (32, 16, 256), jnp.float32)
        _ctx_1024c = jax.random.dirichlet(jax.random.fold_in(_rk, 511), 0.3 * jnp.ones((16,), jnp.float32), (32, 256))
        _ctx_1024t = jnp.einsum('bsk,bkd->bsd', _ctx_1024c, _ctx_1024P)
        _ctx_1024t = _ctx_1024t * jax.lax.rsqrt(jnp.mean(jnp.square(_ctx_1024t)) + 1e-12) * 0.953939
        ctx_1024 = 4.13588e-05 + 0.999923 * (_ctx_1024t + 0.3 * jax.random.normal(jax.random.fold_in(_rk, 611), (32, 256, 256), jnp.float32))
        _validS = jnp.arange(256)[None, :] < _lenS[:, None]
        _validS2 = jnp.arange(256)[None, :] < _lenS2[:, None]
        _causal = jnp.tril(jnp.ones((256, 256), dtype=bool))
        mask_BxSxS2_fk0 = jnp.where(jnp.broadcast_to(_validS2[:, None, :], (32, 256, 256)), 0.0, 1.0).astype(jnp.float32)
        return (x, ctx_1024, mask_BxSxS2_fk0)
    x, ctx_1024, mask_BxSxS2_fk0 = _rec_inputs()

    def _L0_xattn_setup():
        import jax, jax.numpy as jnp
        import numpy as np
        import math
        B, S, D, H, FF = (4, 512, 256, 16, 1024)
        HD = D // H
        EPS = 1e-05

        def _layer_norm(x, g, b):
            m = jnp.mean(x, axis=-1, keepdims=True)
            v = jnp.mean((x - m) ** 2, axis=-1, keepdims=True)
            return (x - m) * jax.lax.rsqrt(v + EPS) * g + b

        def _self_attn(x, mask, Wq, bq, Wk, bk, Wv, bv, Wo, bo):
            b, s, d = x.shape
            q = (x @ Wq.T + bq).reshape(b, s, H, HD)
            k = (x @ Wk.T + bk).reshape(b, s, H, HD)
            v = (x @ Wv.T + bv).reshape(b, s, H, HD)
            score = jnp.einsum('bshd,bthd->bhst', q, k) / math.sqrt(HD)
            score = score + (1.0 - mask[:, None, :, :]) * -1000000000.0
            p = jax.nn.softmax(score, axis=-1)
            o = jnp.einsum('bhst,bthd->bshd', p, v).reshape(b, s, d)
            return o @ Wo.T + bo
        key = jax.random.key(seed)
        ks = jax.random.split(key, 16)
        sd = 0.02
        inp = {'tgt': jax.random.normal(ks[0], (B, S, D), jnp.float32), 'memory': jax.random.normal(ks[1], (B, S, D), jnp.float32), 'mask': jnp.broadcast_to(jnp.tril(jnp.ones((S, S), jnp.float32)), (B, S, S)), 'Wq': jax.random.normal(ks[2], (D, D), jnp.float32) * sd, 'bq': jnp.zeros((D,), jnp.float32), 'Wk': jax.random.normal(ks[3], (D, D), jnp.float32) * sd, 'bk': jnp.zeros((D,), jnp.float32), 'Wv': jax.random.normal(ks[4], (D, D), jnp.float32) * sd, 'bv': jnp.zeros((D,), jnp.float32), 'Wo': jax.random.normal(ks[5], (D, D), jnp.float32) * sd, 'bo': jnp.zeros((D,), jnp.float32), 'Wg': jax.random.normal(ks[6], (D, D), jnp.float32) * sd, 'bg': jnp.zeros((D,), jnp.float32), 'W1': jax.random.normal(ks[7], (FF, D), jnp.float32) * sd, 'b1': jnp.zeros((FF,), jnp.float32), 'W2': jax.random.normal(ks[8], (D, FF), jnp.float32) * sd, 'b2': jnp.zeros((D,), jnp.float32), 'g1': jnp.ones((D,), jnp.float32), 'be1': jnp.zeros((D,), jnp.float32), 'g2': jnp.ones((D,), jnp.float32), 'be2': jnp.zeros((D,), jnp.float32)}
        return inp
    _L0_xattn_all = _L0_xattn_setup()
    _L0_xattn_in = {k: v for k, v in _L0_xattn_all.items() if k in ('Wq', 'bq', 'Wk', 'bk', 'Wv', 'bv', 'Wo', 'bo', 'Wg', 'bg', 'W1', 'b1', 'W2', 'b2', 'g1', 'be1', 'g2', 'be2')}
    del _L0_xattn_all

    def _L1_xattn_setup():
        import jax, jax.numpy as jnp
        import numpy as np
        D_MODEL = 256
        N_HEADS = 16
        D_FF = 1024
        BLOCK = 64
        ROUTER_H = 128
        NEG = -1000000000.0

        def _layernorm(x, g, b, eps=1e-05):
            mu = x.mean(-1, keepdims=True)
            var = ((x - mu) ** 2).mean(-1, keepdims=True)
            return (x - mu) * jax.lax.rsqrt(var + eps) * g + b

        def _block_sparse_self_attn(x, qkv_w, sa_out_w, sa_out_b, r_w1, r_b1, r_w2, r_b2):
            B, S, D = x.shape
            H, Dh = (N_HEADS, D // N_HEADS)
            nb = S // BLOCK
            qkv = x @ qkv_w.T
            q, k, v = jnp.split(qkv, 3, axis=-1)
            q = q.reshape(B, S, H, Dh).transpose(0, 2, 1, 3)
            kh = k.reshape(B, S, H, Dh).transpose(0, 2, 1, 3)
            vh = v.reshape(B, S, H, Dh).transpose(0, 2, 1, 3)
            scores = jnp.einsum('bhqd,bhkd->bhqk', q, kh) / jnp.sqrt(jnp.float32(D))
            block_repr = k.reshape(B, nb, BLOCK, D).mean(axis=2)
            r = jax.nn.relu(block_repr @ r_w1.T + r_b1) @ r_w2.T + r_b2
            keep0 = jax.nn.sigmoid(r[0, :, 0]) > 0.5
            allowed = keep0[:, None] & keep0[None, :]
            allowed_pos = jnp.repeat(jnp.repeat(allowed, BLOCK, 0), BLOCK, 1)
            scores = jnp.where(allowed_pos[None, None], scores, NEG)
            causal = jnp.triu(jnp.ones((S, S), bool), k=1)
            scores = jnp.where(causal[None, None], -jnp.inf, scores)
            p = jax.nn.softmax(scores, axis=-1)
            out = jnp.einsum('bhqk,bhkd->bhqd', p, vh)
            out = out.transpose(0, 2, 1, 3).reshape(B, S, D)
            return out @ sa_out_w.T + sa_out_b

        def _mha_cross(q_in, kv_in, in_w, in_b, out_w, out_b):
            B, S, D = q_in.shape
            M = kv_in.shape[1]
            H, Dh = (N_HEADS, D // N_HEADS)
            wq, wk, wv = jnp.split(in_w, 3, axis=0)
            bq, bk, bv = jnp.split(in_b, 3, axis=0)
            q = (q_in @ wq.T + bq).reshape(B, S, H, Dh).transpose(0, 2, 1, 3)
            k = (kv_in @ wk.T + bk).reshape(B, M, H, Dh).transpose(0, 2, 1, 3)
            v = (kv_in @ wv.T + bv).reshape(B, M, H, Dh).transpose(0, 2, 1, 3)
            scores = jnp.einsum('bhqd,bhkd->bhqk', q, k) / jnp.sqrt(jnp.float32(Dh))
            p = jax.nn.softmax(scores, axis=-1)
            out = jnp.einsum('bhqk,bhkd->bhqd', p, v).transpose(0, 2, 1, 3).reshape(B, S, D)
            return out @ out_w.T + out_b
        key = jax.random.key(seed)
        ks = jax.random.split(key, 24)
        B, S, M, D = (2, 512, 256, D_MODEL)
        s = lambda k, shape, fan: jax.random.normal(k, shape, jnp.float32) * (1.0 / np.sqrt(fan))
        return {'tgt': jax.random.normal(ks[0], (B, S, D), jnp.float32), 'memory': jax.random.normal(ks[1], (B, M, D), jnp.float32), 'qkv_w': s(ks[2], (3 * D, D), D), 'sa_out_w': s(ks[3], (D, D), D), 'sa_out_b': jnp.zeros((D,), jnp.float32), 'r_w1': s(ks[4], (ROUTER_H, D), D), 'r_b1': jnp.zeros((ROUTER_H,), jnp.float32), 'r_w2': s(ks[5], (1, ROUTER_H), ROUTER_H), 'r_b2': jnp.zeros((1,), jnp.float32), 'ca_in_w': s(ks[6], (3 * D, D), D), 'ca_in_b': jnp.zeros((3 * D,), jnp.float32), 'ca_out_w': s(ks[7], (D, D), D), 'ca_out_b': jnp.zeros((D,), jnp.float32), 'ff_w1': s(ks[8], (D_FF, D), D), 'ff_b1': jnp.zeros((D_FF,), jnp.float32), 'ff_w2': s(ks[9], (D, D_FF), D_FF), 'ff_b2': jnp.zeros((D,), jnp.float32), 'n1_g': jnp.ones((D,), jnp.float32), 'n1_b': jnp.zeros((D,), jnp.float32), 'n2_g': jnp.ones((D,), jnp.float32), 'n2_b': jnp.zeros((D,), jnp.float32), 'n3_g': jnp.ones((D,), jnp.float32), 'n3_b': jnp.zeros((D,), jnp.float32)}
    _L1_xattn_all = _L1_xattn_setup()
    _L1_xattn_in = {k: v for k, v in _L1_xattn_all.items() if k in ('qkv_w', 'sa_out_w', 'sa_out_b', 'r_w1', 'r_b1', 'r_w2', 'r_b2', 'ca_in_w', 'ca_in_b', 'ca_out_w', 'ca_out_b', 'ff_w1', 'ff_b1', 'ff_w2', 'ff_b2', 'n1_g', 'n1_b', 'n2_g', 'n2_b', 'n3_g', 'n3_b')}
    del _L1_xattn_all
    return {'x': x, 'ctx_1024': ctx_1024, 'mask_BxSxS2_fk0': mask_BxSxS2_fk0, 'L0_xattn_Wq': _L0_xattn_in['Wq'], 'L0_xattn_bq': _L0_xattn_in['bq'], 'L0_xattn_Wk': _L0_xattn_in['Wk'], 'L0_xattn_bk': _L0_xattn_in['bk'], 'L0_xattn_Wv': _L0_xattn_in['Wv'], 'L0_xattn_bv': _L0_xattn_in['bv'], 'L0_xattn_Wo': _L0_xattn_in['Wo'], 'L0_xattn_bo': _L0_xattn_in['bo'], 'L0_xattn_Wg': _L0_xattn_in['Wg'], 'L0_xattn_bg': _L0_xattn_in['bg'], 'L0_xattn_W1': _L0_xattn_in['W1'], 'L0_xattn_b1': _L0_xattn_in['b1'], 'L0_xattn_W2': _L0_xattn_in['W2'], 'L0_xattn_b2': _L0_xattn_in['b2'], 'L0_xattn_g1': _L0_xattn_in['g1'], 'L0_xattn_be1': _L0_xattn_in['be1'], 'L0_xattn_g2': _L0_xattn_in['g2'], 'L0_xattn_be2': _L0_xattn_in['be2'], 'L1_xattn_qkv_w': _L1_xattn_in['qkv_w'], 'L1_xattn_sa_out_w': _L1_xattn_in['sa_out_w'], 'L1_xattn_sa_out_b': _L1_xattn_in['sa_out_b'], 'L1_xattn_r_w1': _L1_xattn_in['r_w1'], 'L1_xattn_r_b1': _L1_xattn_in['r_b1'], 'L1_xattn_r_w2': _L1_xattn_in['r_w2'], 'L1_xattn_r_b2': _L1_xattn_in['r_b2'], 'L1_xattn_ca_in_w': _L1_xattn_in['ca_in_w'], 'L1_xattn_ca_in_b': _L1_xattn_in['ca_in_b'], 'L1_xattn_ca_out_w': _L1_xattn_in['ca_out_w'], 'L1_xattn_ca_out_b': _L1_xattn_in['ca_out_b'], 'L1_xattn_ff_w1': _L1_xattn_in['ff_w1'], 'L1_xattn_ff_b1': _L1_xattn_in['ff_b1'], 'L1_xattn_ff_w2': _L1_xattn_in['ff_w2'], 'L1_xattn_ff_b2': _L1_xattn_in['ff_b2'], 'L1_xattn_n1_g': _L1_xattn_in['n1_g'], 'L1_xattn_n1_b': _L1_xattn_in['n1_b'], 'L1_xattn_n2_g': _L1_xattn_in['n2_g'], 'L1_xattn_n2_b': _L1_xattn_in['n2_b'], 'L1_xattn_n3_g': _L1_xattn_in['n3_g'], 'L1_xattn_n3_b': _L1_xattn_in['n3_b']}

def reference(x, ctx_1024, mask_BxSxS2_fk0, L0_xattn_Wq, L0_xattn_bq, L0_xattn_Wk, L0_xattn_bk, L0_xattn_Wv, L0_xattn_bv, L0_xattn_Wo, L0_xattn_bo, L0_xattn_Wg, L0_xattn_bg, L0_xattn_W1, L0_xattn_b1, L0_xattn_W2, L0_xattn_b2, L0_xattn_g1, L0_xattn_be1, L0_xattn_g2, L0_xattn_be2, L1_xattn_qkv_w, L1_xattn_sa_out_w, L1_xattn_sa_out_b, L1_xattn_r_w1, L1_xattn_r_b1, L1_xattn_r_w2, L1_xattn_r_b2, L1_xattn_ca_in_w, L1_xattn_ca_in_b, L1_xattn_ca_out_w, L1_xattn_ca_out_b, L1_xattn_ff_w1, L1_xattn_ff_b1, L1_xattn_ff_w2, L1_xattn_ff_b2, L1_xattn_n1_g, L1_xattn_n1_b, L1_xattn_n2_g, L1_xattn_n2_b, L1_xattn_n3_g, L1_xattn_n3_b):
    import jax
    import jax.numpy as jnp

    def _L0_xattn_ref(tgt, memory, mask, Wq, bq, Wk, bk, Wv, bv, Wo, bo, Wg, bg, W1, b1, W2, b2, g1, be1, g2, be2):
        import jax, jax.numpy as jnp
        import numpy as np
        import math
        B, S, D, H, FF = (4, 512, 256, 16, 1024)
        HD = D // H
        EPS = 1e-05

        def _layer_norm(x, g, b):
            m = jnp.mean(x, axis=-1, keepdims=True)
            v = jnp.mean((x - m) ** 2, axis=-1, keepdims=True)
            return (x - m) * jax.lax.rsqrt(v + EPS) * g + b

        def _self_attn(x, mask, Wq, bq, Wk, bk, Wv, bv, Wo, bo):
            b, s, d = x.shape
            q = (x @ Wq.T + bq).reshape(b, s, H, HD)
            k = (x @ Wk.T + bk).reshape(b, s, H, HD)
            v = (x @ Wv.T + bv).reshape(b, s, H, HD)
            score = jnp.einsum('bshd,bthd->bhst', q, k) / math.sqrt(HD)
            score = score + (1.0 - mask[:, None, :, :]) * -1000000000.0
            p = jax.nn.softmax(score, axis=-1)
            o = jnp.einsum('bhst,bthd->bshd', p, v).reshape(b, s, d)
            return o @ Wo.T + bo
        tgt1 = _layer_norm(tgt, g1, be1)
        tgt = tgt + _self_attn(tgt1, mask, Wq, bq, Wk, bk, Wv, bv, Wo, bo)
        tgt = tgt + (memory @ Wg.T + bg)
        tgt1 = _layer_norm(tgt, g2, be2)
        ff = jax.nn.relu(tgt1 @ W1.T + b1) @ W2.T + b2
        return tgt + ff

    def _L1_xattn_ref(tgt, memory, qkv_w, sa_out_w, sa_out_b, r_w1, r_b1, r_w2, r_b2, ca_in_w, ca_in_b, ca_out_w, ca_out_b, ff_w1, ff_b1, ff_w2, ff_b2, n1_g, n1_b, n2_g, n2_b, n3_g, n3_b):
        import jax, jax.numpy as jnp
        import numpy as np
        D_MODEL = 256
        N_HEADS = 16
        D_FF = 1024
        BLOCK = 64
        ROUTER_H = 128
        NEG = -1000000000.0

        def _layernorm(x, g, b, eps=1e-05):
            mu = x.mean(-1, keepdims=True)
            var = ((x - mu) ** 2).mean(-1, keepdims=True)
            return (x - mu) * jax.lax.rsqrt(var + eps) * g + b

        def _block_sparse_self_attn(x, qkv_w, sa_out_w, sa_out_b, r_w1, r_b1, r_w2, r_b2):
            B, S, D = x.shape
            H, Dh = (N_HEADS, D // N_HEADS)
            nb = S // BLOCK
            qkv = x @ qkv_w.T
            q, k, v = jnp.split(qkv, 3, axis=-1)
            q = q.reshape(B, S, H, Dh).transpose(0, 2, 1, 3)
            kh = k.reshape(B, S, H, Dh).transpose(0, 2, 1, 3)
            vh = v.reshape(B, S, H, Dh).transpose(0, 2, 1, 3)
            scores = jnp.einsum('bhqd,bhkd->bhqk', q, kh) / jnp.sqrt(jnp.float32(D))
            block_repr = k.reshape(B, nb, BLOCK, D).mean(axis=2)
            r = jax.nn.relu(block_repr @ r_w1.T + r_b1) @ r_w2.T + r_b2
            keep0 = jax.nn.sigmoid(r[0, :, 0]) > 0.5
            allowed = keep0[:, None] & keep0[None, :]
            allowed_pos = jnp.repeat(jnp.repeat(allowed, BLOCK, 0), BLOCK, 1)
            scores = jnp.where(allowed_pos[None, None], scores, NEG)
            causal = jnp.triu(jnp.ones((S, S), bool), k=1)
            scores = jnp.where(causal[None, None], -jnp.inf, scores)
            p = jax.nn.softmax(scores, axis=-1)
            out = jnp.einsum('bhqk,bhkd->bhqd', p, vh)
            out = out.transpose(0, 2, 1, 3).reshape(B, S, D)
            return out @ sa_out_w.T + sa_out_b

        def _mha_cross(q_in, kv_in, in_w, in_b, out_w, out_b):
            B, S, D = q_in.shape
            M = kv_in.shape[1]
            H, Dh = (N_HEADS, D // N_HEADS)
            wq, wk, wv = jnp.split(in_w, 3, axis=0)
            bq, bk, bv = jnp.split(in_b, 3, axis=0)
            q = (q_in @ wq.T + bq).reshape(B, S, H, Dh).transpose(0, 2, 1, 3)
            k = (kv_in @ wk.T + bk).reshape(B, M, H, Dh).transpose(0, 2, 1, 3)
            v = (kv_in @ wv.T + bv).reshape(B, M, H, Dh).transpose(0, 2, 1, 3)
            scores = jnp.einsum('bhqd,bhkd->bhqk', q, k) / jnp.sqrt(jnp.float32(Dh))
            p = jax.nn.softmax(scores, axis=-1)
            out = jnp.einsum('bhqk,bhkd->bhqd', p, v).transpose(0, 2, 1, 3).reshape(B, S, D)
            return out @ out_w.T + out_b
        x = _layernorm(tgt, n1_g, n1_b)
        tgt = tgt + _block_sparse_self_attn(x, qkv_w, sa_out_w, sa_out_b, r_w1, r_b1, r_w2, r_b2)
        x = _layernorm(tgt, n2_g, n2_b)
        tgt = tgt + _mha_cross(x, memory, ca_in_w, ca_in_b, ca_out_w, ca_out_b)
        x = _layernorm(tgt, n3_g, n3_b)
        ff = jax.nn.relu(x @ ff_w1.T + ff_b1) @ ff_w2.T + ff_b2
        return tgt + ff
    x = _L0_xattn_ref(x, ctx_1024, mask_BxSxS2_fk0, L0_xattn_Wq, L0_xattn_bq, L0_xattn_Wk, L0_xattn_bk, L0_xattn_Wv, L0_xattn_bv, L0_xattn_Wo, L0_xattn_bo, L0_xattn_Wg, L0_xattn_bg, L0_xattn_W1, L0_xattn_b1, L0_xattn_W2, L0_xattn_b2, L0_xattn_g1, L0_xattn_be1, L0_xattn_g2, L0_xattn_be2)
    x = _L1_xattn_ref(x, ctx_1024, L1_xattn_qkv_w, L1_xattn_sa_out_w, L1_xattn_sa_out_b, L1_xattn_r_w1, L1_xattn_r_b1, L1_xattn_r_w2, L1_xattn_r_b2, L1_xattn_ca_in_w, L1_xattn_ca_in_b, L1_xattn_ca_out_w, L1_xattn_ca_out_b, L1_xattn_ff_w1, L1_xattn_ff_b1, L1_xattn_ff_w2, L1_xattn_ff_b2, L1_xattn_n1_g, L1_xattn_n1_b, L1_xattn_n2_g, L1_xattn_n2_b, L1_xattn_n3_g, L1_xattn_n3_b)
    return x

_drawn_inputs = setup_inputs


def setup_inputs(seed=0):
    import zlib

    import numpy as np

    out = dict(_drawn_inputs(seed))
    spreads = {'L0_xattn_bq': (0.0, 0.8),
     'L0_xattn_bk': (0.0, 0.8),
     'L0_xattn_bv': (0.0, 0.1),
     'L0_xattn_bo': (0.0, 0.1),
     'L0_xattn_bg': (0.0, 0.1),
     'L0_xattn_b1': (0.0, 0.1),
     'L0_xattn_b2': (0.0, 0.1),
     'L0_xattn_g1': (1.0, 0.6),
     'L0_xattn_be1': (0.0, 0.681),
     'L0_xattn_g2': (1.0, 0.6),
     'L0_xattn_be2': (0.0, 0.538),
     'L1_xattn_sa_out_b': (0.0, 0.1),
     'L1_xattn_r_b1': (0.0, 0.1),
     'L1_xattn_ca_in_b': (0.0, 0.1),
     'L1_xattn_ca_out_b': (0.0, 0.1),
     'L1_xattn_ff_b1': (0.0, 0.1),
     'L1_xattn_ff_b2': (0.0, 0.1),
     'L1_xattn_n1_g': (1.0, 0.2),
     'L1_xattn_n1_b': (0.0, 0.1),
     'L1_xattn_n2_g': (1.0, 0.2),
     'L1_xattn_n2_b': (0.0, 0.467),
     'L1_xattn_n3_g': (1.0, 0.2),
     'L1_xattn_n3_b': (0.0, 0.1)}
    factors = {'L0_xattn_Wq': 8.0, 'L0_xattn_Wk': 8.0}
    for name, (base, spread) in spreads.items():
        noise = np.random.default_rng([zlib.crc32(name.encode()), seed]).standard_normal(out[name].shape)
        drawn = base * np.exp(spread * noise) if base else spread * noise
        out[name] = jnp.asarray(drawn.astype(out[name].dtype))
    for name, factor in factors.items():
        out[name] = (out[name] * factor).astype(out[name].dtype)
    return out
```

```python
from contextlib import ExitStack

import numpy as np

import concourse.bass as bass
from concourse import mybir

F32 = mybir.dt.float32
F32R = mybir.dt.float32r
BF16 = mybir.dt.bfloat16
FP16 = mybir.dt.float16
ACT = mybir.ActivationFunctionType
ALU = mybir.AluOpType
AX = mybir.AxisListType

P = 128
B, S, D = 32, 256, 256
H, HD = 16, 16
HH = H // 2
TT = S // P
KC = D // P
FF = 1024
NQ = FF // D
BLOCK = 64
NBLK = S // BLOCK
EPS = 1e-5
UNIT = KC * D
QSLOTS = (0, 1, 2, 0, 1, 0)
KSLOTS = (0, 0, 0, 1, 1, 2)
ROWS = len(QSLOTS) * HD
VC = 3 * HD + 1
BLOCKED = 1e30
FUTURE = 3e38

UNITS = (["q0", "k0", "v0", "o0", "g0"] + [f"up0_{i}" for i in range(NQ)] + [f"down0_{i}" for i in range(NQ)]
         + ["q1", "k1", "v1", "o1", "q2", "k2", "v2", "o2"]
         + [f"up1_{i}" for i in range(NQ)] + [f"down1_{i}" for i in range(NQ)])
U = {n: i for i, n in enumerate(UNITS)}
NORM_OF = {"q0": 0, "k0": 0, "v0": 0, "q1": 2, "k1": 2, "v1": 2, "q2": 3}
NORM_OF.update({f"up0_{i}": 1 for i in range(NQ)})
NORM_OF.update({f"up1_{i}": 4 for i in range(NQ)})
SCALE_OF = {"q0": -0.25, "q1": -0.0625, "q2": -0.25}
BIASED = [n for n in UNITS if n in NORM_OF] + ["k2", "v2"]
BCOL = {n: 2 * i for i, n in enumerate(BIASED)}
NBC = 2 * len(BIASED)
GAIN0 = NBC
SHIFT0 = GAIN0 + 2 * 5
RB1, RW2, RB2 = SHIFT0 + 10, SHIFT0 + 11, SHIFT0 + 12
NSMALL = RB2 + 1

USES = {
    0: [("tr0", 0), ("qk0", 1), ("v", 0), ("qk1", 1)],
    1: [("trc", 0), ("tro", 1), ("out", 0), ("tr1", 1)] + [(f"up{q}", 1) for q in range(NQ)]
       + [("down", 0), ("tr2", 1), ("qk0", 0), ("v", 1), ("qk1", 0)],
    2: [("tro", 0), ("out", 1), ("tr3", 0), ("qk0", 1), ("v", 0), ("qk1", 1)],
    3: [("tro", 0), ("out", 1), ("tr4", 0)] + [(f"up{q}", 0) for q in range(NQ)] + [("down", 1)],
}
NU = {k: len(v) for k, v in USES.items()}
IDX = {k: {n: i for i, (n, _) in enumerate(v)} for k, v in USES.items()}
BANK = {k: {n: b for n, b in v} for k, v in USES.items()}
TRS = {0: ["tr0"], 1: ["trc", "tro", "tr1", "tr2"], 2: ["tro", "tr3"], 3: ["tro", "tr4"]}
RING = {(0, 0): 0, (0, 1): 1, (2, 0): 2, (2, 1): 0, (1, 0): 1, (1, 1): 2}
STAGE_AFTER = {0: 1, 1: 2, 2: 3}
FFN_LAYER = {1: 0, 3: 1}
LAST_STEP = H


class Seq:

    def __init__(self, reg, off):
        self.reg, self.off = reg, off

    def __add__(self, n):
        return Seq(self.reg, self.off + n)

    def count(self, per, k):
        n = self.off * per + k
        return n if self.reg is None else self.reg * per + n

    def index(self):
        return self.off if self.reg is None else self.reg + self.off


def wait(eng, sem, value):
    if not isinstance(value, int) or value > 0:
        eng.wait_ge(sem, value)


def filling(slot):
    ffn = ["up0", "up1", "down0", "up2", "down1", "up3", "down2", "down3"]
    if slot == 0:
        return [(4 + n, p, 2) for n, p in enumerate(["tro", "out", "stats3", "norm3", "tr3", "qk0", "v", "qk1"])]
    if slot == 2:
        late = ["tro", "out", "stats1", "norm1", "tr1"] + ffn + ["stats2", "norm2", "tr2", "qk0", "v", "qk1"]
        return [(1, "trc", 1)] + [(4 + n * 12 // len(late), p, 1) for n, p in enumerate(late)]
    early = [(0, "mask", 0), (0, "stats0", 0), (1, "norm0", 0), (2, "tr0", 0), (3, "qk0", 0), (4, "v", 0), (5, "qk1", 0)]
    late = ["tro", "out", "stats4", "norm4", "tr4"] + ffn + ["store"]
    return early + [(5 + n * 11 // len(late), p, 3) for n, p in enumerate(late)]


def program(nc, x, ctx_in, mask, weights, small, rows, rw1, out):
    with ExitStack() as stack:
        def sb(name, shape, dt=F32):
            return stack.enter_context(nc.sbuf_tensor(name, shape, dt))

        def ps(name, shape):
            return stack.enter_context(nc.psum_tensor(name, shape, F32))

        made = {}

        def sem(name):
            if name not in made:
                made[name] = stack.enter_context(nc.semaphore(name))
            return made[name]

        WH = sb("WH", [P, len(UNITS) * UNIT], F32R)
        WL = sb("WL", [P, len(UNITS) * UNIT], F32R)
        QS = [sb(f"QS{r}", [ROWS, HH, S], BF16) for r in range(3)]
        KS = [sb(f"KS{r}", [ROWS, HH, S], BF16) for r in range(3)]
        X = [sb(f"X{n}", [P, TT, D]) for n in range(3)]
        ctx_tok = sb("ctx_tok", [P, TT, D])
        mask_raw = sb("mask_raw", [P, TT, S])
        mask_add = [sb("mask_add0", [P, TT, S]), sb("mask_add1", [P, TT, S])]
        xhat = sb("xhat", [P, TT, D])
        XH, XL = sb("XH", [P, KC, S], F32R), sb("XL", [P, KC, S], F32R)
        CH, CL = sb("CH", [P, KC, S], F32R), sb("CL", [P, KC, S], F32R)
        parts = [sb(f"parts{c}", [P, 3, 2, S], BF16) for c in range(2)]
        tq = sb("tq", [P, 2, S])
        tv = sb("tv", [P, TT, D])
        V = [sb(f"V{a}", [P, TT, H, VC], BF16) for a in range(3)]
        PR = sb("PR", [P, 4, TT, S])
        nmax = sb("nmax", [P, 4, TT])
        PH = [sb(f"PH{n}", [P, KC, TT, P], FP16) for n in range(2)]
        PL = [sb(f"PL{n}", [P, KC, TT, P], FP16) for n in range(2)]
        osum = sb("osum", [P, TT, P])
        orec = sb("orec", [P, TT, HH])
        o_tok = sb("o_tok", [P, TT, D])
        hf = [sb(f"hf{n}", [P, KC, S]) for n in range(2)]
        hh = [sb(f"hh{n}", [P, KC, S], F32R) for n in range(2)]
        hl = [sb(f"hl{n}", [P, KC, S], F32R) for n in range(2)]
        R = sb("R", [P, 5, D])
        ident = sb("ident", [P, P])
        smalls = sb("smalls", [P, NSMALL])
        bcol = sb("bcol", [P, NBC])
        bn = sb("bn", [P, TT, 6])
        mv = sb("mv", [P, TT, 2])
        veps = sb("veps", [P, TT])
        rstd = sb("rstd", [P, TT])
        mhalf = sb("mhalf", [P, TT])
        kmean = sb("kmean", [P, KC, NBLK])
        rhid = sb("rhid", [P, NBLK])
        keep = sb("keep", [P, NBLK])
        keep_q = sb("keep_q", [P, TT])
        router_w1 = sb("router_w1", [P, KC, P])
        router_w2 = sb("router_w2", [P, P])
        stage = PR
        wfull = [hf[0], hf[1]]
        bvb = xhat
        keep_k = o_tok

        SC = [ps(f"SC{n}", [P, TT, S]) for n in range(2)]
        PT = [ps(f"PT{n}", [P, KC, TT, P]) for n in range(2)]
        AV = [ps(f"AV{n}", [P, 512]) for n in range(TT)]
        T = [ps(f"T{n}", [P, 2, S]) for n in range(2)]

        def wait_apart(eng, *waits):
            waits = [(m, v if isinstance(v, int) else eng.to_reg(v)) for m, v in waits]
            eng.wait_ge(sem("small_loaded"), 16)
            for m, v in waits:
                wait(eng, m, v)

        def av(qt, h8):
            return AV[qt][:, h8 * VC:(h8 + 1) * VC]

        def w_in(W, unit, kc, lo=0, n=D):
            at = U[unit] * UNIT + kc * D + lo
            return W[:, at:at + n]

        x_v = x.rearrange("b (t p) d -> b p t d", p=P)
        c_v = ctx_in.rearrange("b (t p) d -> b p t d", p=P)
        m_v = mask.rearrange("b (t p) d -> b p t d", p=P)
        o_v = out.rearrange("b (t p) d -> b p t d", p=P)

        def stream(eng, loop, attn_step, piece):
            def slot(a, seq, prev, fill, drain=False):
                plan = filling(a)
                for s in range(H):
                    attn_step((a, seq), prev, s)
                    for at, name, k in plan:
                        if at == s and k in fill:
                            piece(name, k, *fill[k])

            def zero(n):
                return Seq(None, n)

            def run(k, seq, prev_stage):
                for plan in (filling(0), filling(2), filling(1)):
                    for _, name, kk in plan:
                        if kk == k:
                            piece(name, k, seq, prev_stage)

            def drain(prev):
                for s in range(4):
                    attn_step(None, prev, s)

            def turn(i):
                slot(0, i, (1, i + -1), {2: (i + -1, (3, i + -2))})
                slot(2, i + -1, (0, i), {1: (i, (2, i + -1))})
                slot(1, i, (2, i + -1), {0: (i + 1, (1, i)), 3: (i + -1, (0, i + 1))})

            run(0, zero(0), None)
            slot(0, zero(0), None, {})
            drain((0, zero(0)))
            run(1, zero(0), (0, zero(0)))
            piece("router", None, zero(0), None)
            slot(1, zero(0), (0, zero(0)), {0: (zero(1), (1, zero(0)))})
            slot(0, zero(1), (1, zero(0)), {2: (zero(0), (0, zero(1)))})
            slot(2, zero(0), (0, zero(1)), {1: (zero(1), (2, zero(0)))})
            slot(1, zero(1), (2, zero(0)), {0: (zero(2), (1, zero(1))), 3: (zero(0), (0, zero(2)))})
            with loop(2, B - 1) as i:
                turn(Seq(i, 0))
            n = B - 1
            slot(0, zero(n), (1, zero(n - 1)), {2: (zero(n - 1), (3, zero(n - 2)))})
            slot(2, zero(n - 1), (0, zero(n)), {1: (zero(n), (2, zero(n - 1)))})
            slot(1, zero(n), (2, zero(n - 1)), {3: (zero(n - 1), (1, zero(n)))})
            drain((1, zero(n)))
            run(2, zero(n), (3, zero(n - 1)))
            slot(2, zero(n), (1, zero(n)), {})
            drain((2, zero(n)))
            run(3, zero(n), (2, zero(n)))

        def drained(prev, first):
            return prev is not None and prev[1].reg is None and (
                (prev[0] == 0 and prev[1].off == 0) or (prev[0] == 1 and prev[1].off == B - 1))

        def head(cur, prev, s, lag):
            if s - lag >= 0:
                return None if cur is None else (*cur, s - lag)
            if prev is None or (cur is not None and drained(prev, s)):
                return None
            return (*prev, H + s - lag)

        def before(cur, prev, h, n):
            if h - n >= 0:
                return (*cur, h - n)
            return None if prev is None else (*prev, H + h - n)

        def reader_of_scores(a):
            return sem(f"exp_done{a}") if a == 2 else sem(f"min_done{a}")

        def bank_free(eng, k, name, seq, prev_stage):
            n, bank = IDX[k][name], BANK[k][name]
            earlier = [i for i in range(n) if USES[k][i][1] == bank]
            if earlier:
                wait(eng, sem(f"t{k}_freed"), seq.count(NU[k], earlier[-1] + 1))
            elif prev_stage is not None:
                pk, pseq = prev_stage
                last = max(i for i in range(NU[pk]) if USES[pk][i][1] == bank)
                wait(eng, sem(f"t{pk}_freed"), pseq.count(NU[pk], last + 1))

        def mm_done(k, name, seq):
            return sem(f"t{k}_product"), seq.count(NU[k], IDX[k][name] + 1)

        def freed(k, name, seq):
            return sem(f"t{k}_freed"), seq.count(NU[k], IDX[k][name] + 1)

        def tr_high(k, name, seq):
            return sem(f"t{k}_tr_high"), seq.count(len(TRS[k]), TRS[k].index(name) + 1)

        def norm_stage(n):
            return {0: 0, 1: 1, 2: 1, 3: 2, 4: 3}[n]

        X_OF_NORM = {0: 0, 1: 0, 2: 1, 3: 2, 4: 2}

        def x_ready(eng, n, seq):
            if n == 0:
                wait(eng, sem("x_loaded"), seq.count(16, 16))
            else:
                k, name = {1: (1, "out"), 2: (1, "down"), 3: (2, "out"), 4: (3, "out")}[n]
                wait(eng, *freed(k, name, seq))

        def build_before(a, seq):
            if a == 2:
                return (0, seq + 1) if not (seq.reg is None and seq.off == B - 1) else (1, seq)
            if a == 1:
                if seq.reg is None and seq.off == 0:
                    return (0, seq)
                return (2, seq + -1)
            if seq.reg is None and seq.off == 0:
                return None
            return (1, seq + -1)

        def prev_of(a, seq):
            first = seq.reg is None and seq.off == 0
            last = seq.reg is None and seq.off == B - 1
            if a == 0:
                return None if first else (1, seq + -1)
            if a == 1:
                return (0, seq) if first else (2, seq + -1)
            return (1, seq) if last else (0, seq + 1)

        units = list(UNITS)

        block = stack.enter_context(nc.Block())

        @block.sync
        def _(sp):
            def sp_wait(semaphore, value):
                wait_apart(sp, (semaphore, value))

            sp.dma_start(smalls[:, :], small).then_inc(sem("small_loaded"), 16)
            sp.dma_start(R[:, :, :], rows[:, 0:5, :]).then_inc(sem("rows_loaded"), 16)
            sp.dma_start(xhat[:, 1, :], rows[:, 5, :]).then_inc(sem("bg_loaded"), 16)
            sp.dma_start(router_w1[:, :, :], rw1).then_inc(sem("rw1_loaded"), 16)
            for n in range(len(units)):
                if n >= 4:
                    sp.wait_ge(sem("w_split"), n - 3)
                sp.dma_start(stage[:, n % 4, :, :], weights[n].rearrange("p (a b) -> p a b", a=KC)).then_inc(
                    sem(f"w_loaded{n % 4}"), 16)

            def load_x(seq):
                sp_wait(sem("t1_freed"), (seq + -1).count(NU[1], IDX[1]["down"] + 1))
                sp.dma_start(X[0][:, :, :], x_v[seq.index()]).then_inc(sem("x_loaded"), 16)
                sp_wait(sem("mask_made"), seq.count(1, 0))
                sp.dma_start(mask_raw[:, :, :], m_v[seq.index()]).then_inc(sem("mask_loaded"), 16)

            def load_ctx(seq):
                sp_wait(sem("t1_product"), (seq + -1).count(NU[1], IDX[1]["trc"] + 1))
                sp.dma_start(ctx_tok[:, :, :], c_v[seq.index()]).then_inc(sem("ctx_loaded"), 16)

            def stacks(a, c, seq):
                sp_wait(sem(f"qk_low{a}"), seq.count(2, c + 1))
                last = seq.reg is None and seq.off == B - 1
                if a == 2 and c == 0:
                    sp_wait(sem("scores_done1"), seq.count(H, H))
                elif a == 2 and not last:
                    sp_wait(sem("scores_done0"), (seq + 1).count(H, HH))
                elif a == 2:
                    sp_wait(sem("scores_done2"), seq.count(H, 0))
                elif a == 1 and c == 0:
                    sp_wait(sem("scores_done0"), seq.count(H, H))
                elif a == 1:
                    sp_wait(sem("scores_done2"), (seq + -1).count(H, HH))
                else:
                    if c == 0:
                        sp_wait(sem("scores_done2"), (seq + -2).count(H, H))
                    else:
                        sp_wait(sem("scores_done1"), (seq + -1).count(H, HH))
                    sp_wait(sem("scores_done0"), (seq + -1).count(H, H))
                r = RING[(a, c)]
                for slot, (pq, pk) in enumerate(zip(QSLOTS, KSLOTS)):
                    at = slice(slot * HD, (slot + 1) * HD)
                    sp.dma_start(QS[r][at, :, :], parts[c][:, pq, 0, :]).then_inc(sem(f"stack{a}_{c}"), 16)
                    sp.dma_start(KS[r][at, :, :], parts[c][:, pk, 1, :]).then_inc(sem(f"stack{a}_{c}"), 16)

            def attn_step(cur, prev, s):
                if cur is None:
                    return
                a, seq = cur
                if a == 1 and s == 0 and not (seq.reg is None and seq.off == B - 1):
                    load_x(seq + 1)
                if a == 0 and s == 8 and not (seq.reg is None and seq.off == 0):
                    load_ctx(seq)

            def piece(name, k, seq, prev_stage):
                if name in ("qk0", "qk1"):
                    stacks(k, int(name[2]), seq)
                if name == "store":
                    sp_wait(*freed(3, "down", seq))
                    sp.dma_start(o_v[seq.index()], X[2][:, :, :]).then_inc(sem("stored"), 16)

            load_x(Seq(None, 0))
            load_ctx(Seq(None, 0))
            stream(sp, sp.Fori, attn_step, piece)
            sp.wait_ge(sem("stored"), 16 * B)

        @block.gpsimd
        def _(pool):
            pool.memset(ident[:, :], 0.0).then_inc(sem("pool_zeroed"), 1)
            pool.memset(mask_add[1][:, :, :], 0.0).then_inc(sem("pool_zeroed"), 1)
            pool.memset(mhalf[:, :], -0.5).then_inc(sem("pool_zeroed"), 1)
            for a in range(3):
                pool.memset(V[a][:, :, :, 3 * HD:VC], 1.0).then_inc(sem("ones_set"), 1)
            pool.wait_ge(sem("pool_zeroed"), 3)
            pool.affine_select(out=ident[:, :], in_=ident[:, :], compare_op=ALU.not_equal, fill=1.0, base=0,
                               pattern=[[-1, P]], channel_multiplier=1).then_inc(sem("ident_ready"), 1)
            for t in range(TT):
                pool.affine_select(out=mask_add[1][:, t, :], in_=mask_add[1][:, t, :], compare_op=ALU.is_ge,
                                   fill=FUTURE, base=P * t, pattern=[[-1, S]],
                                   channel_multiplier=1).then_inc(sem("causal_ready"), 1)

            def attn_step(cur, prev, s):
                pass

            def piece(name, k, seq, prev_stage):
                if name == "mask":
                    wait_apart(pool, (sem("mask_loaded"), seq.count(16, 16)), (sem("min_done0"), seq.count(H, 0)))
                    pool.tensor_scalar(mask_add[0][:, :, :], mask_raw[:, :, :], 1.0, -1e9, ALU.subtract,
                                       ALU.mult).then_inc(sem("mask_made"), 1)
                elif name.startswith("stats"):
                    n = int(name[5])
                    wait_apart(pool, (sem(f"ln{n}_moments"), seq.count(1, 1)))
                    pool.tensor_scalar_add(veps[:, :], mv[:, :, 1], EPS).then_inc(sem(f"ln{n}_veps"), 1)
                    wait(pool, sem(f"ln{n}_veps"), seq.count(1, 1))
                    pool.tensor_tensor(rstd[:, :], veps[:, :], mhalf[:, :], ALU.pow).then_inc(sem(f"ln{n}_rstd"), 1)
                elif name.startswith("norm"):
                    n = int(name[4])
                    xn = X[X_OF_NORM[n]]
                    wait(pool, sem(f"ln{n}_xhat"), seq.count(1, 1))
                    row = R[:, n, :].unsqueeze(1).to_broadcast([P, TT, D])
                    pool.tensor_tensor(xn[:, :, :], xn[:, :, :], row, ALU.add).then_inc(sem(f"x_biased{n}"), 1)
                elif name in ("qk0", "qk1"):
                    c = int(name[2])
                    wait(pool, sem(f"qk_mid{k}"), seq.count(2, c + 1))
                    pool.tensor_tensor(parts[c][:, 2, :, :], tq[:, :, :], parts[c][:, 1, :, :],
                                       ALU.subtract).then_inc(sem(f"qk_low{k}"), 1)
                elif name == "v":
                    wait(pool, sem(f"v_mid{k}"), seq.count(1, 1))
                    pool.tensor_tensor(V[k][:, :, :, 2 * HD:3 * HD], tv[:, :, :].rearrange("p t (h f) -> p t h f", f=HD),
                                       V[k][:, :, :, HD:2 * HD], ALU.subtract).then_inc(sem(f"v_low{k}"), 1)
                elif name in ("up0", "up1", "up2", "up3"):
                    q = int(name[2])
                    wait(pool, sem(f"h_high{k}"), seq.count(NQ, q + 1))
                    pool.tensor_tensor(hl[q % 2][:, :, :], hf[q % 2][:, :, :], hh[q % 2][:, :, :],
                                       ALU.subtract).then_inc(sem(f"h_low{k}"), 1)

            stream(pool, pool.Fori, attn_step, piece)

        @block.scalar
        def _(act):
            def attn_step(cur, prev, s):
                at = head(cur, prev, s, 0)
                if at:
                    a, seq, h = at
                    wait(act, sem(f"min_done{a}"), seq.count(H, h + 1))
                    if a == 2:
                        old = before(cur, prev, h, 4)
                        wait(act, sem(f"turned{old[0]}"), old[1].count(H, old[2] + 1))
                    for qt in range(TT):
                        n = P if a == 1 and qt == 0 else S
                        src = SC[h % 2][:, qt, 0:n] if a == 2 else PR[:, h % 4, qt, 0:n]
                        ins = act.activation(PR[:, h % 4, qt, 0:n], src, ACT.Exp,
                                             bias=nmax[:, h % 4, qt:qt + 1], scale=-1.0)
                    ins.then_inc(sem(f"exp_done{a}"), 1)
                at = head(cur, prev, s, 2)
                if at:
                    a, seq, h = at
                    wait(act, sem(f"turned{a}"), seq.count(H, h + 1))
                    old = before((a, seq), prev_of(a, seq), h, 2)
                    if old:
                        wait(act, sem(f"av_done{old[0]}"), old[1].count(H, old[2] + 1))
                    if a == 1:
                        act.activation(PH[h % 2][:, 0, :, :], PT[h % 2][:, 0, :, :], ACT.Copy)
                        act.activation(PH[h % 2][:, 1, 1, :], PT[h % 2][:, 1, 1, :], ACT.Copy).then_inc(
                            sem(f"p_high{a}"), 1)
                    else:
                        act.activation(PH[h % 2][:, :, :, :], PT[h % 2][:, :, :, :], ACT.Copy).then_inc(
                            sem(f"p_high{a}"), 1)

            def piece(name, k, seq, prev_stage):
                if name.startswith("tr"):
                    wait(act, *mm_done(k, name, seq))
                    dst = CH if name == "trc" else XH
                    act.activation(dst[:, :, :], T[BANK[k][name]][:, :, :], ACT.Copy).then_inc(sem(f"t{k}_tr_high"), 1)
                elif name in ("qk0", "qk1"):
                    c = int(name[2])
                    wait(act, *mm_done(k, name, seq))
                    old = build_before(k, seq)
                    if old:
                        wait(act, sem(f"stack{old[0]}_{c}"), old[1].count(192, 192))
                    for side, w in enumerate("qk"):
                        b = BCOL[f"{w}{k}"] + c
                        ins = act.activation(parts[c][:, 0, side, :], T[BANK[k][name]][:, side, :], ACT.Identity,
                                             bias=bcol[:, b:b + 1])
                    ins.then_inc(sem(f"qk_high{k}"), 1)
                elif name == "v":
                    wait(act, *mm_done(k, name, seq))
                    wait(act, sem(f"av_done{k}"), seq.count(H, 0))
                    act.activation(V[k][:, :, :, 0:HD],
                                   T[BANK[k][name]][:, :, :].rearrange("p t (h f) -> p t h f", f=HD),
                                   ACT.Copy).then_inc(sem(f"v_high{k}"), 1)
                elif name in ("up0", "up1", "up2", "up3"):
                    q = int(name[2])
                    wait(act, *mm_done(k, name, seq))
                    if q >= 2:
                        wait(act, sem(f"h_low{k}"), seq.count(NQ, q - 1))
                    for j in range(KC):
                        b = BCOL[f"up{FFN_LAYER[k]}_{q}"] + j
                        ins = act.activation(hf[q % 2][:, j, :], T[BANK[k][name]][:, j, :], ACT.Relu,
                                             bias=bcol[:, b:b + 1])
                    ins.then_inc(sem(f"t{k}_freed"), 1)
                elif name == "router":
                    act.wait_ge(sem("router_hidden"), 1)
                    act.activation(rhid[:, :], T[1][:, 0, 0:NBLK], ACT.Relu,
                                   bias=smalls[:, RB1:RB1 + 1]).then_inc(sem("router_relu"), 1)

            stream(act, act.Fori, attn_step, piece)

        @block.vector
        def _(dve):
            dve.wait_ge(sem("small_loaded"), 16)
            dve.wait_ge(sem("rows_loaded"), 16)
            dve.wait_ge(sem("bg_loaded"), 16)
            dve.tensor_tensor(R[:, 0, :], R[:, 0, :], xhat[:, 1, :], ALU.add).then_inc(sem("row0_summed"), 1)
            for n, u in enumerate(units):
                dve.wait_ge(sem(f"w_loaded{n % 4}"), 16 * (n // 4 + 1))
                st, full = stage[:, n % 4, :, :], wfull[n % 2]
                if n >= 2:
                    dve.wait_ge(sem("w_split"), n - 1)
                for kc in range(KC):
                    g = GAIN0 + 2 * NORM_OF[u] + kc if u in NORM_OF else None
                    scale = SCALE_OF.get(u, 1.0)
                    if g is None:
                        ins = dve.tensor_copy(full[:, kc, :], st[:, kc, :])
                    else:
                        ins = dve.tensor_scalar(full[:, kc, :], st[:, kc, :], smalls[:, g:g + 1], scale,
                                                ALU.mult, ALU.mult)
                ins.then_inc(sem("w_folded"), 1)
                dve.wait_ge(sem("w_folded"), n + 1)
                at = slice(n * UNIT, (n + 1) * UNIT)
                flat = full[:, :, :].rearrange("p a b -> p (a b)")
                dve.tensor_copy(WH[:, at], flat).then_inc(sem("w_high"), 1)
                if u in BCOL:
                    dve.wait_ge(sem("w_high"), n + 1)
                    c0 = BCOL[u]
                    if u in NORM_OF:
                        dve.wait_ge(sem("bias_product"), 1 + [v for v in units if v in NORM_OF].index(u))
                        dve.tensor_tensor(bcol[:, c0:c0 + 2], T[0][:, 0, c0:c0 + 2], smalls[:, c0:c0 + 2],
                                          ALU.add).then_inc(sem("bias_col"), 1)
                    else:
                        dve.tensor_copy(bcol[:, c0:c0 + 2], smalls[:, c0:c0 + 2]).then_inc(sem("bias_col"), 1)
                    nb = 1 + [v for v in units if v in BCOL].index(u)
                    if u in SCALE_OF:
                        dve.wait_ge(sem("bias_col"), nb)
                        dve.tensor_scalar_mul(bcol[:, c0:c0 + 2], bcol[:, c0:c0 + 2],
                                              SCALE_OF[u]).then_inc(sem("bias_scaled"), 1)
                    if u[0] == "v":
                        a = int(u[1])
                        dve.wait_ge(sem("bias_col"), nb)
                        if a:
                            dve.wait_ge(sem("row_product"), a)
                        else:
                            dve.wait_ge(sem("row0_summed"), 1)
                        for kc in range(KC):
                            ins = dve.tensor_copy(bvb[:, kc, 0:P], bcol[:, c0 + kc:c0 + kc + 1].to_broadcast([P, P]))
                        ins.then_inc(sem("bv_spread"), 1)
                if u[0] == "o":
                    a = int(u[1])
                    r = (0, 2, 3)[a]
                    dve.wait_ge(sem("row_product"), a + 1)
                    if a == 0:
                        dve.wait_ge(sem("row0_summed"), 1)
                    dve.tensor_tensor(R[:, r, :], T[1][:, 0, :], R[:, r, :], ALU.add).then_inc(sem("row_ready"), 1)
                dve.wait_ge(sem("w_high"), n + 1)
                dve.tensor_tensor(WL[:, at], flat, WH[:, at], ALU.subtract).then_inc(sem("w_split"), 1)
            dve.wait_ge(sem("w_split"), len(units))
            dve.wait_ge(sem("row_ready"), 3)
            dve.wait_ge(sem("bias_scaled"), 3)
            dve.wait_ge(sem("bias_col"), len(BIASED))
            dve.tensor_copy(keep[:, 0:1], smalls[:, 0:1]).then_inc(sem("start_done"), 1)

            def attn_step(cur, prev, s):
                at = head(cur, prev, s, 0)
                if at:
                    a, seq, h = at
                    scores = (sem(f"scores_done{a}"), seq.count(H, h + 1))
                    if a == 2:
                        wait(dve, *scores)
                        dve.tensor_reduce(nmax[:, h % 4, :], SC[h % 2][:, :, :], axis=AX.X,
                                          op=ALU.min).then_inc(sem("min_done2"), 1)
                    else:
                        waits = [scores]
                        old = before(cur, prev, h, 4)
                        if old:
                            waits.append((sem(f"turned{old[0]}"), old[1].count(H, old[2] + 1)))
                        if h == 0:
                            waits.append((sem("mask_made"), seq.count(1, 1)) if a == 0 else
                                         (sem("sparse_ready"), TT))
                        wait_apart(dve, *waits)
                        for qt in range(TT):
                            n = P if a == 1 and qt == 0 else S
                            ins = dve.tensor_tensor_reduce(
                                out=PR[:, h % 4, qt, 0:n], in0=SC[h % 2][:, qt, 0:n],
                                in1=mask_add[a][:, qt, 0:n], scale=1.0, scalar=3.4e38, op0=ALU.add, op1=ALU.min,
                                accum_out=nmax[:, h % 4, qt:qt + 1])
                        ins.then_inc(sem(f"min_done{a}"), 1)
                at = head(cur, prev, s, 2)
                if at:
                    a, seq, h = at
                    wait(dve, sem(f"p_high{a}"), seq.count(H, h + 1))
                    if a == 1:
                        dve.tensor_tensor(PL[h % 2][:, 0, :, :], PT[h % 2][:, 0, :, :], PH[h % 2][:, 0, :, :],
                                          ALU.subtract)
                        dve.tensor_tensor(PL[h % 2][:, 1, 1, :], PT[h % 2][:, 1, 1, :], PH[h % 2][:, 1, 1, :],
                                          ALU.subtract).then_inc(sem(f"p_low{a}"), 1)
                    else:
                        dve.tensor_tensor(PL[h % 2][:, :, :, :], PT[h % 2][:, :, :, :], PH[h % 2][:, :, :, :],
                                          ALU.subtract).then_inc(sem(f"p_low{a}"), 1)
                at = head(cur, prev, s, 4) if cur is not None or s < 3 else None
                if cur is None and s == 3:
                    at = (*prev, H - 1)
                if at and at[2] % HH == HH - 1:
                    a, seq, h = at
                    c = h // HH
                    wait(dve, sem(f"av_done{a}"), seq.count(H, h + 1))
                    for qt in range(TT):
                        src = AV[qt][:, 0:HH * VC].rearrange("p (h c) -> p h c", c=VC)[:, :, 0:3 * HD]
                        ins = dve.tensor_reduce(osum[:, qt, :].rearrange("p (h f) -> p h f", f=HD),
                                                src.rearrange("p h (r f) -> p h f r", r=3), axis=AX.X, op=ALU.add)
                        den = AV[qt][:, 0:HH * VC].rearrange("p (h c) -> p h c", c=VC)[:, :, 3 * HD]
                        ins = dve.reciprocal(orec[:, qt, :], den)
                    ins.then_inc(sem(f"o_sum{a}"), 1)
                    wait(dve, sem(f"o_sum{a}"), seq.count(2, c + 1))
                    for qt in range(TT):
                        ins = dve.tensor_tensor(
                            o_tok[:, qt, c * P:(c + 1) * P].rearrange("p (h f) -> p h f", f=HD),
                            osum[:, qt, :].rearrange("p (h f) -> p h f", f=HD),
                            orec[:, qt, :].unsqueeze(2).to_broadcast([P, HH, HD]), ALU.mult)
                    ins.then_inc(sem(f"o_ready{a}"), 1)

            def piece(name, k, seq, prev_stage):
                if name.startswith("stats"):
                    n = int(name[5])
                    xn = X[X_OF_NORM[n]]
                    x_ready(dve, n, seq)
                    for t in range(TT):
                        ins = dve.bn_stats(bn[:, t, :], xn[:, t, :])
                    ins.then_inc(sem(f"ln{n}_stats"), 1)
                    wait_apart(dve, (sem(f"ln{n}_stats"), seq.count(1, 1)))
                    for t in range(TT):
                        ins = dve.bn_aggr(mv[:, t, :], bn[:, t, :])
                    ins.then_inc(sem(f"ln{n}_moments"), 1)
                elif name.startswith("norm"):
                    n = int(name[4])
                    xn = X[X_OF_NORM[n]]
                    wait(dve, sem(f"ln{n}_rstd"), seq.count(1, 1))
                    for t in range(TT):
                        ins = dve.tensor_scalar(xhat[:, t, :], xn[:, t, :], mv[:, t, 0:1], rstd[:, t:t + 1],
                                                ALU.subtract, ALU.mult)
                    ins.then_inc(sem(f"ln{n}_xhat"), 1)
                elif name.startswith("tr"):
                    wait(dve, *tr_high(k, name, seq))
                    high, low = (CH, CL) if name == "trc" else (XH, XL)
                    dve.tensor_tensor(low[:, :, :], T[BANK[k][name]][:, :, :], high[:, :, :],
                                      ALU.subtract).then_inc(sem(f"t{k}_freed"), 1)
                elif name in ("qk0", "qk1"):
                    c = int(name[2])
                    wait(dve, sem(f"qk_high{k}"), seq.count(2, c + 1))
                    if c:
                        wait(dve, sem(f"qk_low{k}"), seq.count(2, 1))
                    else:
                        old = build_before(k, seq)
                        if old:
                            wait(dve, sem(f"qk_low{old[0]}"), old[1].count(2, 2))
                    for side, w in enumerate("qk"):
                        b = BCOL[f"{w}{k}"] + c
                        ins = dve.scalar_tensor_tensor(tq[:, side, :], T[BANK[k][name]][:, side, :],
                                                       bcol[:, b:b + 1], parts[c][:, 0, side, :], ALU.add,
                                                       ALU.subtract)
                    ins.then_inc(sem(f"t{k}_freed"), 1)
                    wait(dve, *freed(k, name, seq))
                    dve.tensor_copy(parts[c][:, 1, :, :], tq[:, :, :]).then_inc(sem(f"qk_mid{k}"), 1)
                elif name == "v":
                    wait(dve, sem(f"v_high{k}"), seq.count(1, 1))
                    old = build_before(k, seq)
                    if old:
                        wait(dve, sem(f"v_low{old[0]}"), old[1].count(1, 1))
                    dve.tensor_tensor(tv[:, :, :].rearrange("p t (h f) -> p t h f", f=HD),
                                      T[BANK[k][name]][:, :, :].rearrange("p t (h f) -> p t h f", f=HD),
                                      V[k][:, :, :, 0:HD], ALU.subtract).then_inc(sem(f"t{k}_freed"), 1)
                    wait(dve, *freed(k, name, seq))
                    dve.tensor_copy(V[k][:, :, :, HD:2 * HD],
                                    tv[:, :, :].rearrange("p t (h f) -> p t h f", f=HD)).then_inc(sem(f"v_mid{k}"), 1)
                elif name == "out":
                    n = {1: 0, 2: 2, 3: 3}[k]
                    wait(dve, *mm_done(k, name, seq))
                    wait(dve, sem(f"x_biased{n}"), seq.count(1, 1))
                    src = X[{1: 0, 2: 1, 3: 2}[k]]
                    dst = X[{1: 0, 2: 2, 3: 2}[k]]
                    if k == 2:
                        wait(dve, sem("stored"), seq.count(16, 0))
                    dve.tensor_tensor(dst[:, :, :], T[BANK[k][name]][:, :, :], src[:, :, :],
                                      ALU.add).then_inc(sem(f"t{k}_freed"), 1)
                elif name in ("up0", "up1", "up2", "up3"):
                    q = int(name[2])
                    wait(dve, *freed(k, name, seq))
                    if q >= 2:
                        wait(dve, sem(f"down_part{k}"), seq.count(2, q - 1))
                    dve.tensor_copy(hh[q % 2][:, :, :], hf[q % 2][:, :, :]).then_inc(sem(f"h_high{k}"), 1)
                elif name == "down3":
                    n = {1: 1, 3: 4}[k]
                    wait(dve, *mm_done(k, "down", seq))
                    wait(dve, sem(f"x_biased{n}"), seq.count(1, 1))
                    src, dst = {1: (X[0], X[1]), 3: (X[2], X[2])}[k]
                    dve.tensor_tensor(dst[:, :, :], T[BANK[k]["down"]][:, :, :], src[:, :, :],
                                      ALU.add).then_inc(sem(f"t{k}_freed"), 1)
                elif name == "router":
                    dve.tensor_copy(router_w2[:, :], smalls[:, RW2:RW2 + 1].to_broadcast([P, P])).then_inc(
                        sem("w2_spread"), 1)
                    dve.wait_ge(sem("qk_low1"), 2)
                    for c in range(KC):
                        for n in range(NBLK):
                            ins = dve.tensor_reduce(kmean[:, c, n:n + 1],
                                                    parts[c][:, :, 1, n * BLOCK:(n + 1) * BLOCK],
                                                    axis=AX.XY, op=ALU.add)
                    ins.then_inc(sem("k_sums"), 1)
                    dve.wait_ge(sem("k_sums"), 1)
                    dve.tensor_scalar_mul(kmean[:, :, :], kmean[:, :, :], 1.0 / BLOCK).then_inc(sem("k_means"), 1)
                    dve.wait_ge(sem("router_score"), 1)
                    dve.tensor_scalar(keep[:, :], T[1][:, 1, 0:NBLK], smalls[:, RB2:RB2 + 1], 0.0, ALU.add,
                                      ALU.is_gt).then_inc(sem("keep_steps"), 1)
                    dve.wait_ge(sem("keep_steps"), 1)
                    dve.wait_ge(sem("causal_ready"), TT)
                    dve.tensor_copy(keep_k[:, 0, :].rearrange("p (n t) -> p n t", t=BLOCK),
                                    keep[:, :].unsqueeze(2).to_broadcast([P, NBLK, BLOCK]))
                    for t in range(TT):
                        for half in range(2):
                            at = slice(half * BLOCK, (half + 1) * BLOCK)
                            n = 2 * t + half
                            ins = dve.tensor_copy(keep_q[at, t:t + 1], keep[at, n:n + 1])
                    ins.then_inc(sem("keep_steps"), 1)
                    dve.wait_ge(sem("keep_steps"), 2)
                    for t in range(TT):
                        dve.tensor_scalar(tv[:, t, :], keep_k[:, 0, :], keep_q[:, t:t + 1], -BLOCKED, ALU.mult,
                                          ALU.mult).then_inc(sem("keep_steps"), 1)
                        dve.wait_ge(sem("keep_steps"), 3 + 2 * t)
                        dve.tensor_scalar_add(tv[:, t, :], tv[:, t, :], BLOCKED).then_inc(sem("keep_steps"), 1)
                        dve.wait_ge(sem("keep_steps"), 4 + 2 * t)
                        dve.tensor_tensor(mask_add[1][:, t, :], mask_add[1][:, t, :], tv[:, t, :],
                                          ALU.max).then_inc(sem("sparse_ready"), 1)

            stream(dve, dve.Fori, attn_step, piece)

        @block.tensor
        def _(pe):
            pe.wait_ge(sem("small_loaded"), 16)
            for n, u in enumerate(units):
                if u in NORM_OF:
                    pe.wait_ge(sem(f"w_loaded{n % 4}"), 16 * (n // 4 + 1))
                    if n:
                        pe.wait_ge(sem("bias_col"), len([v for v in units[:n] if v in BCOL]))
                    s0 = SHIFT0 + 2 * NORM_OF[u]
                    for oc in range(KC):
                        for kc in range(KC):
                            ins = pe.matmul(T[0][:, 0, BCOL[u] + oc:BCOL[u] + oc + 1],
                                            stage[:, n % 4, kc, oc * P:(oc + 1) * P], smalls[:, s0 + kc:s0 + kc + 1],
                                            start=(kc == 0), stop=(kc == KC - 1))
                    ins.then_inc(sem("bias_product"), 1)
                if u[0] == "o":
                    pe.wait_ge(sem(f"w_loaded{n % 4}"), 16 * (n // 4 + 1))
                    pe.wait_ge(sem("bv_spread"), int(u[1]) + 1)
                    if int(u[1]):
                        pe.wait_ge(sem("row_ready"), int(u[1]))
                    for kc in range(KC):
                        ins = pe.matmul(T[1][:, 0, :], bvb[:, kc, 0:P], stage[:, n % 4, kc, :],
                                        start=(kc == 0), stop=(kc == KC - 1))
                    ins.then_inc(sem("row_product"), 1)
            pe.wait_ge(sem("start_done"), 1)
            pe.wait_ge(sem("ident_ready"), 1)
            pe.wait_ge(sem("ones_set"), 3)

            def three(out, stat, move, first, last, lone=True):
                (sh, sl), (mh, ml) = stat, move
                pe.matmul(out, sh, mh, start=first, stop=False, skip_group_check=not lone)
                pe.matmul(out, sh, ml, start=False, stop=False, skip_group_check=not lone)
                return pe.matmul(out, sl, mh, start=False, stop=last, skip_group_check=not lone)

            def features(out, unit, oc, xh, xl):
                for kc in range(KC):
                    ins = three(out, (w_in(WH, unit, kc, oc * P, P), w_in(WL, unit, kc, oc * P, P)),
                                (xh[:, kc, :], xl[:, kc, :]), kc == 0, kc == KC - 1)
                return ins

            def tokens(out, t, terms):
                for n, (unit, xh, xl) in enumerate(terms):
                    at = slice(t * P, (t + 1) * P)
                    for kc in range(KC):
                        ins = three(out, (xh[:, kc, at], xl[:, kc, at]), (w_in(WH, unit, kc), w_in(WL, unit, kc)),
                                    n == 0 and kc == 0, n == len(terms) - 1 and kc == KC - 1)
                return ins

            def attn_step(cur, prev, s):
                at = head(cur, prev, s, 0)
                if at:
                    a, seq, h = at
                    c, h8, r = h // HH, h % HH, RING[(a, h // HH)]
                    if h8 == 0:
                        wait(pe, sem(f"stack{a}_{c}"), seq.count(192, 192))
                    old = before(cur, prev, h, 2)
                    if old:
                        wait(pe, reader_of_scores(old[0]), old[1].count(H, old[2] + 1))
                    for qt in range(TT):
                        n = P if a == 1 and qt == 0 else S
                        ins = pe.matmul(SC[h % 2][:, qt, 0:n], QS[r][:, h8, qt * P:(qt + 1) * P],
                                        KS[r][:, h8, 0:n], start=True, stop=True)
                    ins.then_inc(sem(f"scores_done{a}"), 1)
                at = head(cur, prev, s, 2)
                if at:
                    a, seq, h = at
                    wait(pe, sem(f"exp_done{a}"), seq.count(H, h + 1))
                    old = before((a, seq), prev_of(a, seq), h, 2)
                    if old:
                        wait(pe, sem(f"p_low{old[0]}"), old[1].count(H, old[2] + 1))
                    for qt in range(TT):
                        for kc in range(1 if a == 1 and qt == 0 else KC):
                            ins = pe.transpose(PT[h % 2][:, kc, qt, :], PR[:, h % 4, qt, kc * P:(kc + 1) * P],
                                               ident[:, :])
                    ins.then_inc(sem(f"turned{a}"), 1)
                at = head(cur, prev, s, 3)
                if at:
                    a, seq, h = at
                    c, h8 = h // HH, h % HH
                    if h == 0:
                        wait(pe, sem(f"v_low{a}"), seq.count(1, 1))
                    if h8 == 0:
                        if c:
                            wait(pe, sem(f"o_ready{a}"), seq.count(2, 1))
                        else:
                            old = prev_of(a, seq)
                            if old:
                                wait(pe, sem(f"o_ready{old[0]}"), old[1].count(2, 2))
                    wait(pe, sem(f"p_low{a}"), seq.count(H, h + 1))
                    for qt in range(TT):
                        nk = 1 if a == 1 and qt == 0 else KC
                        for kc in range(nk):
                            for half in (PH, PL):
                                ins = pe.matmul(av(qt, h8), half[h % 2][:, kc, qt, :], V[a][:, kc, h, :],
                                                start=(kc == 0 and half is PH), stop=(kc == nk - 1 and half is PL))
                    ins.then_inc(sem(f"av_done{a}"), 1)

            def turn_tile(src, bank):
                for t in range(TT):
                    for kc in range(KC):
                        ins = pe.transpose(T[bank][:, kc, t * P:(t + 1) * P], src[:, t, kc * P:(kc + 1) * P],
                                           ident[:, :])
                return ins

            def piece(name, k, seq, prev_stage):
                if name.startswith("tr"):
                    if name == "trc":
                        wait(pe, sem("ctx_loaded"), seq.count(16, 16))
                        src = ctx_tok
                    elif name == "tro":
                        wait(pe, sem(f"o_ready{k - 1}"), seq.count(2, 2))
                        src = o_tok
                    else:
                        wait(pe, sem(f"ln{name[2]}_xhat"), seq.count(1, 1))
                        src = xhat
                    bank_free(pe, k, name, seq, prev_stage)
                    turn_tile(src, BANK[k][name]).then_inc(sem(f"t{k}_product"), 1)
                elif name in ("qk0", "qk1"):
                    c = int(name[2])
                    bank_free(pe, k, name, seq, prev_stage)
                    wait(pe, *freed(k, TRS[k][-1], seq))
                    bank = T[BANK[k][name]]
                    features(bank[:, 0, :], f"q{k}", c, XH, XL)
                    kx = (CH, CL) if k == 2 else (XH, XL)
                    features(bank[:, 1, :], f"k{k}", c, *kx).then_inc(sem(f"t{k}_product"), 1)
                elif name == "v":
                    bank_free(pe, k, name, seq, prev_stage)
                    kx = (CH, CL) if k == 2 else (XH, XL)
                    for t in range(TT):
                        ins = tokens(T[BANK[k][name]][:, t, :], t, [(f"v{k}", *kx)])
                    ins.then_inc(sem(f"t{k}_product"), 1)
                elif name == "out":
                    bank_free(pe, k, name, seq, prev_stage)
                    wait(pe, *freed(k, "tro", seq))
                    terms = [(f"o{k - 1}", XH, XL)] + ([("g0", CH, CL)] if k == 1 else [])
                    for t in range(TT):
                        ins = tokens(T[BANK[k][name]][:, t, :], t, terms)
                    ins.then_inc(sem(f"t{k}_product"), 1)
                elif name in ("up0", "up1", "up2", "up3"):
                    bank_free(pe, k, name, seq, prev_stage)
                    if name == "up0":
                        wait(pe, *freed(k, "tr1" if k == 1 else "tr4", seq))
                    for oc in range(KC):
                        ins = features(T[BANK[k][name]][:, oc, :], f"up{FFN_LAYER[k]}_{name[2]}", oc, XH, XL)
                    ins.then_inc(sem(f"t{k}_product"), 1)
                elif name.startswith("down"):
                    q = int(name[4])
                    if q == 0:
                        bank_free(pe, k, "down", seq, prev_stage)
                    wait(pe, sem(f"h_low{k}"), seq.count(NQ, q + 1))
                    for t in range(TT):
                        at = slice(t * P, (t + 1) * P)
                        for kc in range(KC):
                            unit = f"down{FFN_LAYER[k]}_{q}"
                            ins = three(T[BANK[k]["down"]][:, t, :], (hh[q % 2][:, kc, at], hl[q % 2][:, kc, at]),
                                        (w_in(WH, unit, kc), w_in(WL, unit, kc)),
                                        q == 0 and t == 0 and kc == 0, q == NQ - 1 and kc == KC - 1, lone=False)
                    if q < 2:
                        ins.then_inc(sem(f"down_part{k}"), 1)
                    elif q == NQ - 1:
                        ins.then_inc(sem(f"t{k}_product"), 1)
                elif name == "router":
                    pe.wait_ge(sem("rw1_loaded"), 16)
                    pe.wait_ge(sem("k_means"), 1)
                    for c in range(KC):
                        ins = pe.matmul(T[1][:, 0, 0:NBLK], router_w1[:, c, :], kmean[:, c, :], start=(c == 0),
                                        stop=(c == KC - 1))
                    ins.then_inc(sem("router_hidden"), 1)
                    pe.wait_ge(sem("router_relu"), 1)
                    pe.wait_ge(sem("w2_spread"), 1)
                    pe.matmul(T[1][:, 1, 0:NBLK], router_w2[:, :], rhid[:, :], start=True,
                              stop=True).then_inc(sem("router_score"), 1)

            stream(pe, pe.Fori, attn_step, piece)


def kernel(**inputs):
    import numpy as _np
    import concourse.bacc as _bacc
    from concourse import mybir as _mybir
    from concourse.bass_utils import run_bass_kernel_spmd as _run

    def l0(n):
        return _np.asarray(inputs["L0_xattn_" + n])

    def l1(n):
        return _np.asarray(inputs["L1_xattn_" + n])

    def by_feature(w):
        return w.reshape(KC, HH, HD, -1).transpose(0, 2, 1, 3).reshape(D, -1)

    def unit(w):
        return w.T.reshape(KC, P, D).transpose(1, 0, 2).reshape(P, UNIT)

    def cols(v):
        return v.reshape(-1, P).T

    zero = _np.zeros(D, _np.float32)
    qkv, ca, cab = l1("qkv_w"), l1("ca_in_w"), l1("ca_in_b")
    w = {"q0": by_feature(l0("Wq")), "k0": by_feature(l0("Wk")), "v0": l0("Wv"), "o0": l0("Wo"), "g0": l0("Wg"),
         "q1": by_feature(qkv[0:D]), "k1": by_feature(qkv[D:2 * D]), "v1": qkv[2 * D:], "o1": l1("sa_out_w"),
         "q2": by_feature(ca[0:D]), "k2": by_feature(ca[D:2 * D]), "v2": ca[2 * D:], "o2": l1("ca_out_w")}
    b = {"q0": by_feature(l0("bq")), "k0": by_feature(l0("bk")), "v0": l0("bv"), "q1": zero, "k1": zero, "v1": zero,
         "q2": by_feature(cab[0:D]), "k2": by_feature(cab[D:2 * D]), "v2": cab[2 * D:]}
    for layer, (w1, b1, w2) in enumerate([(l0("W1"), l0("b1"), l0("W2")), (l1("ff_w1"), l1("ff_b1"), l1("ff_w2"))]):
        for q in range(NQ):
            at = slice(q * D, (q + 1) * D)
            w[f"up{layer}_{q}"], b[f"up{layer}_{q}"] = w1[at], b1[at]
            w[f"down{layer}_{q}"] = w2[:, at]
    norms = [(l0("g1"), l0("be1")), (l0("g2"), l0("be2")), (l1("n1_g"), l1("n1_b")), (l1("n2_g"), l1("n2_b")),
             (l1("n3_g"), l1("n3_b"))]
    small = _np.concatenate([cols(b[n]) for n in BIASED] + [cols(g) for g, _ in norms] + [cols(s) for _, s in norms]
                            + [cols(l1("r_b1")), cols(l1("r_w2")), _np.broadcast_to(l1("r_b2"), (P, 1))], axis=1)
    rows = _np.stack([l0("bo"), l0("b2"), l1("sa_out_b"), l1("ca_out_b"), l1("ff_b2"), l0("bg")])
    rw1 = by_feature(l1("r_w1").T).reshape(KC, P, P).transpose(1, 0, 2)
    arrays = {
        "x": inputs["x"], "ctx_in": inputs["ctx_1024"], "mask": inputs["mask_BxSxS2_fk0"],
        "weights": _np.stack([unit(w[n]) for n in UNITS]), "small": small,
        "rows": _np.broadcast_to(rows, (P, 6, D)), "rw1": rw1,
    }
    arrays = {n: _np.ascontiguousarray(a) for n, a in arrays.items()}
    nc = _bacc.Bacc("TRN2", target_bir_lowering=False, num_devices=1, dynamic_dma_scratch_size=1024)
    args = [nc.dram_tensor(n, a.shape, _mybir.dt.from_np(a.dtype), kind="ExternalInput").ap()
            for n, a in arrays.items()]
    out = nc.dram_tensor("out", (B, S, D), _mybir.dt.float32, kind="ExternalOutput").ap()
    program(nc, *args, out)
    r = _run(nc, [arrays], core_ids=[0])
    return r.results[0]["out"]
```

```python
from contextlib import ExitStack

import numpy as np

import concourse.bass as bass
from concourse import mybir

F32 = mybir.dt.float32
F32R = mybir.dt.float32r
BF16 = mybir.dt.bfloat16
FP16 = mybir.dt.float16
ACT = mybir.ActivationFunctionType
ALU = mybir.AluOpType
AX = mybir.AxisListType

P = 128
B, S, D = 32, 256, 256
H, HD = 16, 16
HH = H // 2
TT = S // P
KC = D // P
FF = 1024
NQ = FF // D
BLOCK = 64
NBLK = S // BLOCK
EPS = 1e-5
UNIT = KC * D
QSLOTS = (0, 1, 2, 0, 1, 0)
KSLOTS = (0, 0, 0, 1, 1, 2)
ROWS = len(QSLOTS) * HD
VC = 3 * HD + 1
BLOCKED = 1e30
FUTURE = 3e38

UNITS = (["q0", "k0", "v0", "o0", "g0"] + [f"up0_{i}" for i in range(NQ)] + [f"down0_{i}" for i in range(NQ)]
         + ["q1", "k1", "v1", "o1", "q2", "k2", "v2", "o2"]
         + [f"up1_{i}" for i in range(NQ)] + [f"down1_{i}" for i in range(NQ)])
U = {n: i for i, n in enumerate(UNITS)}
NORM_OF = {"q0": 0, "k0": 0, "v0": 0, "q1": 2, "k1": 2, "v1": 2, "q2": 3}
NORM_OF.update({f"up0_{i}": 1 for i in range(NQ)})
NORM_OF.update({f"up1_{i}": 4 for i in range(NQ)})
SCALE_OF = {"q0": -0.25, "q1": -0.0625, "q2": -0.25}
BIASED = [n for n in UNITS if n in NORM_OF] + ["k2", "v2"]
BCOL = {n: 2 * i for i, n in enumerate(BIASED)}
NBC = 2 * len(BIASED)
GAIN0 = NBC
SHIFT0 = GAIN0 + 2 * 5
RB1, RW2, RB2 = SHIFT0 + 10, SHIFT0 + 11, SHIFT0 + 12
NSMALL = RB2 + 1

USES = {
    0: [("tr0", 2), ("qk0", 2), ("v", 2), ("qk1", 2)],
    1: [("trc", 0), ("tro", 1), ("out", 0), ("tr1", 1)] + [(f"up{q}", 1) for q in range(NQ)]
       + [("down", 0), ("tr2", 2), ("qk0", 2), ("v", 2), ("qk1", 2)],
    2: [("tro", 2), ("out", 2), ("tr3", 2), ("v", 2), ("qk0", 2), ("qk1", 2)],
    3: [("tro", 0), ("out", 1), ("tr4", 0)] + [(f"up{q}", 0) for q in range(NQ)] + [("down", 1)],
}
NU = {k: len(v) for k, v in USES.items()}
IDX = {k: {n: i for i, (n, _) in enumerate(v)} for k, v in USES.items()}
BANK = {k: {n: b for n, b in v} for k, v in USES.items()}
TRS = {0: ["tr0"], 1: ["trc", "tro", "tr1", "tr2"], 2: ["tro", "tr3"], 3: ["tro", "tr4"]}
RING = {(0, 0): 0, (0, 1): 1, (1, 0): 2, (1, 1): 0, (2, 0): 1, (2, 1): 2}
FFN_LAYER = {1: 0, 3: 1}
EXP_LAG, TURN_LAG, SPLIT_LAG, AV_LAG, OUT_LAG = 1, 2, 3, 4, 5
RING3 = 3
STAGES = RING3
GROUP = 4
NG = H // GROUP

HEADS = [(0, 0), (1, -1), (2, -2)]
TURN = len(HEADS) * H

PIECES = {
    0: [(-26, "mask"), (-21, "stats0"), (-21, "norm0"), (-20, "tr0"), (-18, "qk0"), (-16, "v"), (-14, "qk1")],
    1: [(21, "trc"), (23, "outg"), (23, "tro"), (24, "out"), (24, "stats1"), (25, "norm1"), (26, "tr1"),
        (27, "up0"), (29, "up1"), (30, "down0"), (32, "up2"), (33, "down1"), (35, "up3"), (37, "down2"),
        (42, "down3"), (42, "stats2"), (43, "norm2"), (44, "tr2"), (46, "qk0"), (49, "v"), (52, "qk1")],
    2: [(63, "carry_ctx"), (86, "tro"), (88, "out"), (98, "stats3"), (101, "norm3"), (103, "tr3"), (105, "v"),
        (106, "qk0"), (112, "qk1"), (127, "carry_x")],
    3: [(150, "tro"), (151, "out"), (152, "stats4"), (153, "norm4"), (154, "tr4"), (155, "up0"), (156, "up1"),
        (157, "down0"), (157, "up2"), (158, "down1"), (158, "up3"), (161, "down2"), (164, "down3")],
}


def in_turn(wanted):
    return [(w, -(at // TURN)) for at, w in sorted(wanted, key=lambda x: x[0] % TURN)]


def when(k, name):
    return next(at for at, n in PIECES[k] if n == name)


FIRST_PIECE = {(1, "out"): "outg", (1, "down"): "down0", (3, "down"): "down0"}
BANK_USES = [in_turn([(when(k, FIRST_PIECE.get((k, n), n)), (k, n)) for k in USES for n, b in USES[k] if b == bank])
             for bank in range(3)]
FFNS = in_turn([(when(k, "up0"), k) for k in FFN_LAYER])
BUILDS = in_turn([(when(k, "qk0"), k) for k in range(3)])
NORMS = in_turn([(when(k, f"norm{n}"), n) for n, k in enumerate([0, 1, 1, 2, 3])])


class Seq:

    def __init__(self, reg, off):
        self.reg, self.off = reg, off

    def __add__(self, n):
        return Seq(self.reg, self.off + n)

    def count(self, per, k):
        n = self.off * per + k
        return n if self.reg is None else self.reg * per + n

    def index(self):
        return self.off if self.reg is None else self.reg + self.off


def wait(eng, sem, value):
    if not isinstance(value, int) or value > 0:
        eng.wait_ge(sem, value)


def program(nc, x, ctx_in, mask, weights, small, rows, rw1, out):
    with ExitStack() as stack:
        def sb(name, shape, dt=F32):
            return stack.enter_context(nc.sbuf_tensor(name, shape, dt))

        def ps(name, shape):
            return stack.enter_context(nc.psum_tensor(name, shape, F32))

        made = {}

        def sem(name):
            if name not in made:
                made[name] = stack.enter_context(nc.semaphore(name))
            return made[name]

        WH = sb("WH", [P, len(UNITS) * UNIT], F32R)
        WL = sb("WL", [P, len(UNITS) * UNIT], F32R)
        QS = [sb(f"QS{r}", [ROWS, HH, S], BF16) for r in range(3)]
        KS = [sb(f"KS{r}", [ROWS, HH, S], BF16) for r in range(3)]
        X = [sb(f"X{n}", [P, TT, D]) for n in range(5)]
        ctx_tok = sb("ctx_tok", [P, TT, D])
        mask_add = [sb("mask_add0", [P, TT, S]), sb("mask_add1", [P, TT, S])]
        xhat = sb("xhat", [P, TT, D])
        XH, XL = [[sb(f"X{w}{n}", [P, KC, S], F32R) for n in range(2)] for w in "HL"]
        CH, CL = [[sb(f"C{w}{n}", [P, KC, S], F32R) for n in range(2)] for w in "HL"]
        parts = [sb(f"parts{c}", [P, 3, 2, S], BF16) for c in range(2)]
        rest = sb("rest", [P, TT, D])
        V = [sb(f"V{a}", [P, TT, H, VC], BF16) for a in range(3)]
        PR = sb("PR", [P, RING3, TT, S])
        nmax = sb("nmax", [P, RING3, TT])
        PH = [sb(f"PH{n}", [P, KC * TT, P], FP16) for n in range(RING3)]
        PL = [sb(f"PL{n}", [P, KC * TT, P], FP16) for n in range(RING3)]
        osum = sb("osum", [P, TT * GROUP, HD])
        orec = sb("orec", [P, TT * GROUP])
        o_tok = sb("o_tok", [P, TT, D])
        hf = sb("hf", [P, KC, S])
        hh = [sb(f"hh{n}", [P, KC, S], F32R) for n in range(2)]
        hl = [sb(f"hl{n}", [P, KC, S], F32R) for n in range(2)]
        R = sb("R", [P, 5, D])
        ident = sb("ident", [P, P])
        smalls = sb("smalls", [P, NSMALL])
        bcol = sb("bcol", [P, NBC])
        bn = sb("bn", [P, TT, 6])
        mv = sb("mv", [P, TT, 2])
        veps = sb("veps", [P, TT])
        rstd = sb("rstd", [P, TT])
        mhalf = sb("mhalf", [P, TT])
        no_mask = sb("no_mask", [P, 1])
        kmean = sb("kmean", [P, KC, NBLK])
        rhid = sb("rhid", [P, NBLK])
        keep = sb("keep", [P, NBLK])
        keep_q = sb("keep_q", [P, TT])
        stage = PR
        wfull = [hf, X[3]]
        bvb = xhat
        keep_k = xhat
        router_w1 = X[4][:, 0, :].rearrange("p (c f) -> p c f", c=KC)
        router_w2 = X[4][:, 1, 0:P]

        SC = [ps(f"SC{n}", [P, TT, S]) for n in range(2)]
        PT = [ps(f"PT{n}", [P, KC * TT, P]) for n in range(2)]
        AV = ps("AV", [P, TT * GROUP, VC])
        T = [ps(f"T{n}", [P, 2, S]) for n in range(3)]

        def wait_apart(eng, *waits):
            waits = [(m, v if isinstance(v, int) else eng.to_reg(v)) for m, v in waits]
            eng.wait_ge(sem("small_loaded"), 16)
            for m, v in waits:
                wait(eng, m, v)

        def w_in(W, unit, kc, lo=0, n=D):
            at = U[unit] * UNIT + kc * D + lo
            return W[:, at:at + n]

        def block_of(kc, qt):
            return qt if kc == 0 else KC * TT - 1 - qt

        def blocks(a):
            return slice(0, KC * TT - (a == 1))

        x_v = x.rearrange("b (t p) d -> b p t d", p=P)
        c_v = ctx_in.rearrange("b (t p) d -> b p t d", p=P)
        m_v = mask.rearrange("b (t p) d -> b p t d", p=P)
        o_v = out.rearrange("b (t p) d -> b p t d", p=P)

        def exists(seq):
            return seq.reg is not None or 0 <= seq.off < B

        def back(order, what, seq):
            at = [w for w, _ in order].index(what)
            turn = seq + -order[at][1]
            for _ in range(4 * len(order)):
                at -= 1
                if at < 0:
                    at, turn = at + len(order), turn + -1
                if exists(turn + order[at][1]):
                    return order[at][0], turn + order[at][1]
            return None

        def stream(eng, loop, order, piece):
            def turn(i):
                prev = back(HEADS, 0, i) if exists(i + -3) else None
                work = [(at % TURN, name, k, i + -(at // TURN)) for k in PIECES for at, name in PIECES[k]]
                if i.reg is None and i.off == 1:
                    work.append((5, "router", None, Seq(None, 0)))
                work.sort(key=lambda w: w[0])
                for n, (a, off) in enumerate(HEADS):
                    cur = (a, i + off) if exists(i + off) else None
                    for s in range(H):
                        for part in order:
                            if part is not PIECES:
                                part(cur, prev, s)
                                continue
                            for at, name, k, seq in work:
                                if at == H * n + s and exists(seq):
                                    piece(name, k, seq)
                    prev = cur

            for n in range(-1, 3):
                turn(Seq(None, n))
            with loop(3, B - 1) as i:
                turn(Seq(i, 0))
            for n in range(B - 1, B + 3):
                turn(Seq(None, n))

        def head(cur, prev, s, lag):
            if s - lag >= 0:
                return None if cur is None else (*cur, s - lag)
            return None if prev is None else (*prev, H + s - lag)

        slot_of = {a: n for n, (a, _) in enumerate(HEADS)}

        def place(a, h):
            return (H * slot_of[a] + h) % RING3

        def before(a, seq, h, n):
            if h - n >= 0:
                return a, seq, h - n
            old = back(HEADS, a, seq)
            if old is None:
                return None
            at, turn = slot_of[a], seq + -dict(HEADS)[a]
            follows = HEADS[at - 1][0] == old[0] and (turn + (HEADS[at - 1][1] - (at == 0))).off == old[1].off
            return (*old, H + h - n) if follows else (*old, H - 1)

        def low_before(k, name, seq):
            names = {0: ["qk0", "v", "qk1"], 1: ["qk0", "v", "qk1"], 2: ["v", "qk0", "qk1"]}
            n = names[k].index(name) - 1
            if n < 0:
                old = back(BUILDS, k, seq)
                if old is None:
                    return sem("qk_low0"), 0
                (k, seq), n = old, 2
            name = names[k][n]
            if name == "v":
                return sem(f"v_low{k}"), seq.count(1, 1)
            return sem(f"qk_low{k}"), seq.count(2, int(name[2]) + 1)

        def bank_free(eng, k, name, seq):
            old = back(BANK_USES[BANK[k][name]], (k, name), seq)
            if old:
                (k, name), seq = old
                wait(eng, *freed(k, name, seq))

        def acts(k, name):
            return int(BANK[k][name] == 2)

        def mm_done(k, name, seq):
            return sem(f"t{k}_product"), seq.count(NU[k], IDX[k][name] + 1)

        def freed(k, name, seq):
            return sem(f"t{k}_freed"), seq.count(NU[k], IDX[k][name] + 1)

        def tr_high(k, name, seq):
            return sem(f"t{k}_tr_high"), seq.count(len(TRS[k]), TRS[k].index(name) + 1)

        X_OF_NORM = {0: 0, 1: 1, 2: 2, 3: 3, 4: 4}
        TR_OF_NORM = {0: (0, "tr0"), 1: (1, "tr1"), 2: (1, "tr2"), 3: (2, "tr3"), 4: (3, "tr4")}

        def x_ready(eng, n, seq):
            if n == 0:
                wait(eng, sem("x_loaded"), seq.count(16, 16))
            else:
                k, name = {1: (1, "out"), 2: (1, "down"), 3: (2, "out"), 4: (3, "out")}[n]
                wait(eng, *freed(k, name, seq))

        units = list(UNITS)
        normed = [u for u in units if u in NORM_OF]
        biased = [u for u in units if u in BCOL]
        bias_banks = (0, 2)

        block = stack.enter_context(nc.Block())

        @block.sync
        def _(sp):
            def sp_wait(semaphore, value):
                wait_apart(sp, (semaphore, value))

            sp.dma_start(smalls[:, :], small).then_inc(sem("small_loaded"), 16)
            sp.dma_start(R[:, :, :], rows[:, 0:5, :]).then_inc(sem("rows_loaded"), 16)
            sp.dma_start(xhat[:, 1, :], rows[:, 5, :]).then_inc(sem("bg_loaded"), 16)
            sp.dma_start(router_w1, rw1).then_inc(sem("rw1_loaded"), 16)
            for n in range(len(units)):
                if n >= STAGES:
                    sp.wait_ge(sem("w_high"), n - STAGES + 1)
                sp.dma_start(stage[:, n % STAGES, :, :], weights[n].rearrange("p (a b) -> p a b", a=KC)).then_inc(
                    sem(f"w_loaded{n % STAGES}"), 16)

            def load_x(seq):
                sp_wait(*freed(1, "out", seq + -1))
                sp.dma_start(X[0][:, :, :], x_v[seq.index()]).then_inc(sem("x_loaded"), 16)

            def load_mask(seq):
                sp_wait(sem("min_done0"), seq.count(H, 0))
                sp.dma_start(mask_add[0][:, :, :], m_v[seq.index()]).then_inc(sem("mask_loaded"), 16)

            def load_ctx(seq):
                sp_wait(*mm_done(1, "trc", seq + -1))
                sp.dma_start(ctx_tok[:, :, :], c_v[seq.index()]).then_inc(sem("ctx_loaded"), 16)

            def stacks(a, c, seq):
                sp_wait(sem(f"qk_low{a}"), seq.count(2, c + 1))
                at = 2 * [w for w, _ in HEADS].index(a) + c
                turn = seq + -dict(HEADS)[a]
                for n in (at - 3, at - 6, at - 9):
                    old, off = HEADS[n % 6 // 2]
                    user = turn + (n // 6 + off)
                    if exists(user):
                        sp_wait(sem(f"scores_done{old}"), user.count(H, H if n % 2 else HH))
                        break
                r = RING[(a, c)]
                for slot, (pq, pk) in enumerate(zip(QSLOTS, KSLOTS)):
                    at = slice(slot * HD, (slot + 1) * HD)
                    sp.dma_start(QS[r][at, :, :], parts[c][:, pq, 0, :]).then_inc(sem(f"stack{a}_{c}"), 16)
                    sp.dma_start(KS[r][at, :, :], parts[c][:, pk, 1, :]).then_inc(sem(f"stack{a}_{c}"), 16)

            PLAN = {
                (0, 0): [("stack", 1, 0, -1)],
                (0, 8): [("stack", 1, 1, -1)],
                (1, 0): [("mask", 1), ("stack", 2, 0, -2)],
                (1, 5): [("store", -3)],
                (1, 7): [("ctx", 1)],
                (1, 8): [("x", 1), ("stack", 2, 1, -2)],
                (2, 0): [("stack", 0, 0, 1)],
                (2, 8): [("stack", 0, 1, 1)],
            }

            def step(a, s, i):
                for what, *args, off in PLAN.get((a, s), []):
                    seq = i + off
                    if not exists(seq):
                        continue
                    if what == "stack":
                        stacks(*args, seq)
                    elif what == "store":
                        sp_wait(*freed(3, "down", seq))
                        sp.dma_start(o_v[seq.index()], X[4][:, :, :]).then_inc(sem("stored"), 16)
                    else:
                        {"mask": load_mask, "ctx": load_ctx, "x": load_x}[what](seq)

            def turn(i):
                for a, _ in HEADS:
                    for s in range(H):
                        step(a, s, i)

            for n in range(-1, 3):
                turn(Seq(None, n))
            with sp.Fori(3, B - 1) as i:
                turn(Seq(i, 0))
            for n in range(B - 1, B + 3):
                turn(Seq(None, n))
            sp.wait_ge(sem("stored"), 16 * B)

        @block.gpsimd
        def _(pool):
            pool.memset(ident[:, :], 0.0).then_inc(sem("pool_zeroed"), 1)
            pool.memset(mask_add[1][:, :, :], 0.0).then_inc(sem("pool_zeroed"), 1)
            pool.memset(mhalf[:, :], -0.5).then_inc(sem("pool_zeroed"), 1)
            pool.memset(no_mask[:, :], 0.0).then_inc(sem("pool_zeroed"), 1)
            for a in range(3):
                pool.memset(V[a][:, :, :, 3 * HD:VC], 1.0).then_inc(sem("ones_set"), 1)
            pool.wait_ge(sem("pool_zeroed"), 4)
            pool.affine_select(out=ident[:, :], in_=ident[:, :], compare_op=ALU.not_equal, fill=1.0, base=0,
                               pattern=[[-1, P]], channel_multiplier=1).then_inc(sem("ident_ready"), 1)
            for t in range(TT):
                pool.affine_select(out=mask_add[1][:, t, :], in_=mask_add[1][:, t, :], compare_op=ALU.is_ge,
                                   fill=FUTURE, base=P * t, pattern=[[-1, S]],
                                   channel_multiplier=1).then_inc(sem("causal_ready"), 1)

            for n in range(len(units)):
                at = slice(n * UNIT, (n + 1) * UNIT)
                pool.wait_ge(sem("w_high"), n + 1)
                pool.tensor_tensor(WL[:, at], wfull[n % 2][:, :, :].rearrange("p a b -> p (a b)"), WH[:, at],
                                   ALU.subtract).then_inc(sem("w_split"), 1)

            def piece(name, k, seq):
                if name == "mask":
                    wait_apart(pool, (sem("mask_loaded"), seq.count(16, 16)))
                    pool.tensor_scalar(mask_add[0][:, :, :], mask_add[0][:, :, :], 1.0, -1e9, ALU.subtract,
                                       ALU.mult).then_inc(sem("mask_made"), 1)
                elif name == "carry_ctx":
                    wait_apart(pool, freed(1, "trc", seq), mm_done(2, "qk1", seq + -1))
                    pool.tensor_copy(CH[1][:, :, :], CH[0][:, :, :])
                    pool.tensor_copy(CL[1][:, :, :], CL[0][:, :, :]).then_inc(sem("ctx_carried"), 1)
                elif name == "carry_x":
                    wait(pool, sem("ln3_xhat"), seq.count(1, 1))
                    wait(pool, sem("stored"), seq.count(16, 0))
                    row = R[:, 3, :].unsqueeze(1).to_broadcast([P, TT, D])
                    pool.tensor_tensor(X[4][:, :, :], X[3][:, :, :], row, ALU.add).then_inc(sem("x_biased3"), 1)
                elif name.startswith("stats"):
                    n = int(name[5])
                    wait_apart(pool, (sem(f"ln{n}_moments"), seq.count(1, 1)))
                    pool.tensor_scalar_add(veps[:, :], mv[:, :, 1], EPS).then_inc(sem(f"ln{n}_veps"), 1)
                    wait(pool, sem(f"ln{n}_veps"), seq.count(1, 1))
                    pool.tensor_tensor(rstd[:, :], veps[:, :], mhalf[:, :], ALU.pow).then_inc(sem(f"ln{n}_rstd"), 1)
                elif name.startswith("norm"):
                    n = int(name[4])
                    if n == 3:
                        return
                    xn = X[X_OF_NORM[n]]
                    wait(pool, sem(f"ln{n}_xhat"), seq.count(1, 1))
                    row = R[:, n, :].unsqueeze(1).to_broadcast([P, TT, D])
                    pool.tensor_tensor(xn[:, :, :], xn[:, :, :], row, ALU.add).then_inc(sem(f"x_biased{n}"), 1)
                elif name in ("qk0", "qk1"):
                    c = int(name[2])
                    wait_apart(pool, freed(k, name, seq))
                    pool.tensor_copy(parts[c][:, 1, :, :], rest[:, :, :]).then_inc(sem(f"qk_mid{k}"), 1)
                    wait(pool, sem(f"qk_mid{k}"), seq.count(2, c + 1))
                    pool.tensor_tensor(parts[c][:, 2, :, :], rest[:, :, :], parts[c][:, 1, :, :],
                                       ALU.subtract).then_inc(sem(f"qk_low{k}"), 1)
                elif name == "v":
                    wait_apart(pool, freed(k, name, seq))
                    pool.tensor_copy(V[k][:, :, :, HD:2 * HD],
                                     rest[:, :, :].rearrange("p t (h f) -> p t h f", f=HD)).then_inc(sem(f"v_mid{k}"), 1)
                    wait(pool, sem(f"v_mid{k}"), seq.count(1, 1))
                    pool.tensor_tensor(V[k][:, :, :, 2 * HD:3 * HD], rest[:, :, :].rearrange("p t (h f) -> p t h f", f=HD),
                                       V[k][:, :, :, HD:2 * HD], ALU.subtract).then_inc(sem(f"v_low{k}"), 1)
                elif name in ("up0", "up1", "up2", "up3"):
                    q = int(name[2])
                    wait(pool, sem(f"h_high{k}"), seq.count(NQ, q + 1))
                    pool.tensor_tensor(hl[q % 2][:, :, :], hf[:, :, :], hh[q % 2][:, :, :],
                                       ALU.subtract).then_inc(sem(f"h_low{k}"), 1)

            stream(pool, pool.Fori, [PIECES], piece)

        @block.scalar
        def _(act):
            def high(cur, prev, s):
                at = head(cur, prev, s, SPLIT_LAG)
                if at:
                    a, seq, h = at
                    wait(act, sem(f"turned{a}"), seq.count(H, h + 1))
                    old = before(a, seq, h, RING3)
                    if old:
                        wait(act, sem(f"av_done{old[0]}"), old[1].count(H, old[2] + 1))
                    act.activation(PH[place(a, h)][:, blocks(a), :], PT[h % 2][:, blocks(a), :],
                                   ACT.Copy).then_inc(sem(f"p_high{a}"), 1)

            def exps(cur, prev, s):
                at = head(cur, prev, s, EXP_LAG)
                if at:
                    a, seq, h = at
                    wait(act, sem(f"min_done{a}"), seq.count(H, h + 1))
                    for qt in range(TT):
                        n = P if a == 1 and qt == 0 else S
                        src = PR[:, place(a, h), qt, 0:n]
                        ins = act.activation(PR[:, place(a, h), qt, 0:n], src, ACT.Exp,
                                             bias=nmax[:, place(a, h), qt:qt + 1], scale=-1.0)
                    ins.then_inc(sem(f"exp_done{a}"), 1)

            def piece(name, k, seq):
                if name.startswith("tr"):
                    wait(act, *mm_done(k, name, seq))
                    dst = CH[0] if name == "trc" else XH[acts(k, name)]
                    if name == "trc":
                        wait(act, sem("ctx_carried"), seq.count(1, 0))
                    act.activation(dst[:, :, :], T[BANK[k][name]][:, :, :], ACT.Copy).then_inc(sem(f"t{k}_tr_high"), 1)
                elif name in ("qk0", "qk1"):
                    c = int(name[2])
                    wait(act, *mm_done(k, name, seq))
                    old = back(BUILDS, k, seq)
                    if old:
                        wait(act, sem(f"stack{old[0]}_{c}"), old[1].count(192, 192))
                    for side, w in enumerate("qk"):
                        b = BCOL[f"{w}{k}"] + c
                        ins = act.activation(parts[c][:, 0, side, :], T[BANK[k][name]][:, side, :], ACT.Identity,
                                             bias=bcol[:, b:b + 1])
                    ins.then_inc(sem(f"qk_high{k}"), 1)
                elif name == "v":
                    wait(act, *mm_done(k, name, seq))
                    wait(act, sem(f"av_done{k}"), seq.count(H, 0))
                    act.activation(V[k][:, :, :, 0:HD],
                                   T[BANK[k][name]][:, :, :].rearrange("p t (h f) -> p t h f", f=HD),
                                   ACT.Copy).then_inc(sem(f"v_high{k}"), 1)
                elif name in ("up0", "up1", "up2", "up3"):
                    q = int(name[2])
                    wait(act, *mm_done(k, name, seq))
                    if q:
                        wait(act, sem(f"h_low{k}"), seq.count(NQ, q))
                    else:
                        old = back(FFNS, k, seq)
                        if old:
                            wait(act, sem(f"h_low{old[0]}"), old[1].count(NQ, NQ))
                    for j in range(KC):
                        b = BCOL[f"up{FFN_LAYER[k]}_{q}"] + j
                        ins = act.activation(hf[:, j, :], T[BANK[k][name]][:, j, :], ACT.Relu,
                                             bias=bcol[:, b:b + 1])
                    ins.then_inc(sem(f"t{k}_freed"), 1)
                    if q >= 2:
                        wait(act, sem(f"down_part{k}"), seq.count(2, q - 1))
                    wait(act, *freed(k, name, seq))
                    act.activation(hh[q % 2][:, :, :], hf[:, :, :], ACT.Copy).then_inc(sem(f"h_high{k}"), 1)
                elif name == "router":
                    act.wait_ge(sem("router_hidden"), 1)
                    act.activation(rhid[:, :], T[1][:, 0, 0:NBLK], ACT.Relu,
                                   bias=smalls[:, RB1:RB1 + 1]).then_inc(sem("router_relu"), 1)

            stream(act, act.Fori, [high, exps, PIECES], piece)

        @block.vector
        def _(dve):
            dve.wait_ge(sem("small_loaded"), 16)
            dve.wait_ge(sem("rows_loaded"), 16)
            dve.wait_ge(sem("bg_loaded"), 16)
            dve.tensor_tensor(R[:, 0, :], R[:, 0, :], xhat[:, 1, :], ALU.add).then_inc(sem("row0_summed"), 1)
            for n, u in enumerate(units):
                dve.wait_ge(sem(f"w_loaded{n % STAGES}"), 16 * (n // STAGES + 1))
                st, full = stage[:, n % STAGES, :, :], wfull[n % 2]
                if n >= 2:
                    dve.wait_ge(sem("w_split"), n - 1)
                for kc in range(KC):
                    g = GAIN0 + 2 * NORM_OF[u] + kc if u in NORM_OF else None
                    scale = SCALE_OF.get(u, 1.0)
                    if g is None:
                        ins = dve.tensor_copy(full[:, kc, :], st[:, kc, :])
                    else:
                        ins = dve.tensor_scalar(full[:, kc, :], st[:, kc, :], smalls[:, g:g + 1], scale,
                                                ALU.mult, ALU.mult)
                ins.then_inc(sem("w_folded"), 1)
                dve.wait_ge(sem("w_folded"), n + 1)
                at = slice(n * UNIT, (n + 1) * UNIT)
                flat = full[:, :, :].rearrange("p a b -> p (a b)")
                if u in BCOL:
                    c0 = BCOL[u]
                    if u in NORM_OF:
                        m = normed.index(u)
                        dve.wait_ge(sem("bias_product"), 1 + m)
                        dve.tensor_tensor(bcol[:, c0:c0 + 2], T[bias_banks[m % 2]][:, 0, c0:c0 + 2], smalls[:, c0:c0 + 2],
                                          ALU.add).then_inc(sem("bias_col"), 1)
                    else:
                        dve.tensor_copy(bcol[:, c0:c0 + 2], smalls[:, c0:c0 + 2]).then_inc(sem("bias_col"), 1)
                    nb = 1 + [v for v in units if v in BCOL].index(u)
                    if u in SCALE_OF:
                        dve.wait_ge(sem("bias_col"), nb)
                        dve.tensor_scalar_mul(bcol[:, c0:c0 + 2], bcol[:, c0:c0 + 2],
                                              SCALE_OF[u]).then_inc(sem("bias_scaled"), 1)
                    if u[0] == "v":
                        a = int(u[1])
                        dve.wait_ge(sem("bias_col"), nb)
                        if a:
                            dve.wait_ge(sem("row_product"), a)
                        else:
                            dve.wait_ge(sem("row0_summed"), 1)
                        for kc in range(KC):
                            ins = dve.tensor_copy(bvb[:, kc, 0:P], bcol[:, c0 + kc:c0 + kc + 1].to_broadcast([P, P]))
                        ins.then_inc(sem("bv_spread"), 1)
                if u[0] == "o":
                    a = int(u[1])
                    r = (0, 2, 3)[a]
                    dve.wait_ge(sem("row_product"), a + 1)
                    if a == 0:
                        dve.wait_ge(sem("row0_summed"), 1)
                    dve.tensor_tensor(R[:, r, :], T[1][:, 0, :], R[:, r, :], ALU.add).then_inc(sem("row_ready"), 1)
                dve.tensor_copy(WH[:, at], flat).then_inc(sem("w_high"), 1)
            dve.wait_ge(sem("w_split"), len(units))
            dve.wait_ge(sem("row_ready"), 3)
            dve.wait_ge(sem("bias_scaled"), 3)
            dve.wait_ge(sem("bias_col"), len(BIASED))
            dve.tensor_copy(keep[:, 0:1], smalls[:, 0:1]).then_inc(sem("start_done"), 1)

            def minimum(cur, prev, s):
                at = head(cur, prev, s, 0)
                if at:
                    a, seq, h = at
                    scores = (sem(f"scores_done{a}"), seq.count(H, h + 1))
                    waits = [scores]
                    old = before(a, seq, h, RING3)
                    if old:
                        waits.append((sem(f"turned{old[0]}"), old[1].count(H, old[2] + 1)))
                    if h == 0:
                        waits.append({0: (sem("mask_made"), seq.count(1, 1)), 1: (sem("sparse_ready"), TT),
                                      2: (sem("pool_zeroed"), 4)}[a])
                    wait_apart(dve, *waits)
                    for qt in range(TT):
                        n = P if a == 1 and qt == 0 else S
                        ins = dve.tensor_tensor_reduce(
                            out=PR[:, place(a, h), qt, 0:n], in0=SC[h % 2][:, qt, 0:n],
                            in1=no_mask[:, 0:1].to_broadcast([P, n]) if a == 2 else mask_add[a][:, qt, 0:n], scale=1.0,
                            scalar=3.4e38, op0=ALU.add, op1=ALU.min,
                            accum_out=nmax[:, place(a, h), qt:qt + 1])
                    ins.then_inc(sem(f"min_done{a}"), 1)

            def sums(cur, prev, s):
                out = head(cur, prev, s, OUT_LAG)
                if out and out[2] % GROUP == GROUP - 1:
                    a, seq, h = out
                    wait(dve, sem(f"av_done{a}"), seq.count(H, h + 1))
                    old = before(a, seq, h, GROUP)
                    if old:
                        wait(dve, sem(f"o_ready{old[0]}"), old[1].count(NG, old[2] // GROUP + 1))
                    dve.reciprocal(orec[:, :], AV[:, :, 3 * HD])
                    dve.tensor_reduce(osum[:, :, :], AV[:, :, 0:3 * HD].rearrange("p g (r f) -> p g f r", r=3),
                                      axis=AX.X, op=ALU.add).then_inc(sem(f"o_sum{a}"), 1)

            def low_half(cur, prev, s):
                at = head(cur, prev, s, SPLIT_LAG)
                if at:
                    a, seq, h = at
                    wait(dve, sem(f"p_high{a}"), seq.count(H, h + 1))
                    low, turned, high = PL[place(a, h)], PT[h % 2], PH[place(a, h)]
                    at = blocks(a)
                    dve.tensor_tensor(low[:, at, :], turned[:, at, :], high[:, at, :],
                                      ALU.subtract).then_inc(sem(f"p_low{a}"), 1)

            def outputs(cur, prev, s):
                out = head(cur, prev, s, OUT_LAG)
                if out and out[2] % GROUP == GROUP - 1:
                    a, seq, h = out
                    g = h // GROUP
                    wait(dve, sem(f"o_sum{a}"), seq.count(NG, g + 1))
                    if g == 0:
                        old = back(HEADS, a, seq)
                        if old:
                            wait(dve, *mm_done(old[0] + 1, "tro", old[1]))
                    dve.tensor_tensor(
                        o_tok[:, :, g * GROUP * HD:(g + 1) * GROUP * HD].rearrange("p t (h f) -> p t h f", f=HD),
                        osum[:, :, :].rearrange("p (t h) f -> p t h f", h=GROUP),
                        orec[:, :].rearrange("p (t h) -> p t h", h=GROUP).unsqueeze(3).to_broadcast([P, TT, GROUP, HD]),
                        ALU.mult).then_inc(sem(f"o_ready{a}"), 1)

            def piece(name, k, seq):
                if name.startswith("stats"):
                    n = int(name[5])
                    xn = X[X_OF_NORM[n]]
                    x_ready(dve, n, seq)
                    for t in range(TT):
                        ins = dve.bn_stats(bn[:, t, :], xn[:, t, :])
                    ins.then_inc(sem(f"ln{n}_stats"), 1)
                    wait_apart(dve, (sem(f"ln{n}_stats"), seq.count(1, 1)))
                    for t in range(TT):
                        ins = dve.bn_aggr(mv[:, t, :], bn[:, t, :])
                    ins.then_inc(sem(f"ln{n}_moments"), 1)
                elif name.startswith("norm"):
                    n = int(name[4])
                    xn = X[X_OF_NORM[n]]
                    wait(dve, sem(f"ln{n}_rstd"), seq.count(1, 1))
                    old = back(NORMS, n, seq)
                    if old:
                        wait(dve, *mm_done(*TR_OF_NORM[old[0]], old[1]))
                    for t in range(TT):
                        ins = dve.tensor_scalar(xhat[:, t, :], xn[:, t, :], mv[:, t, 0:1], rstd[:, t:t + 1],
                                                ALU.subtract, ALU.mult)
                    ins.then_inc(sem(f"ln{n}_xhat"), 1)
                elif name.startswith("tr"):
                    wait(dve, *tr_high(k, name, seq))
                    high, low = (CH[0], CL[0]) if name == "trc" else (XH[acts(k, name)], XL[acts(k, name)])
                    dve.tensor_tensor(low[:, :, :], T[BANK[k][name]][:, :, :], high[:, :, :],
                                      ALU.subtract).then_inc(sem(f"t{k}_freed"), 1)
                elif name in ("qk0", "qk1"):
                    c = int(name[2])
                    wait(dve, sem(f"qk_high{k}"), seq.count(2, c + 1))
                    wait(dve, *low_before(k, name, seq))
                    for side, w in enumerate("qk"):
                        b = BCOL[f"{w}{k}"] + c
                        ins = dve.scalar_tensor_tensor(rest[:, side, :], T[BANK[k][name]][:, side, :],
                                                       bcol[:, b:b + 1], parts[c][:, 0, side, :], ALU.add,
                                                       ALU.subtract)
                    ins.then_inc(sem(f"t{k}_freed"), 1)
                elif name == "v":
                    wait(dve, sem(f"v_high{k}"), seq.count(1, 1))
                    wait(dve, *low_before(k, name, seq))
                    dve.tensor_tensor(rest[:, :, :].rearrange("p t (h f) -> p t h f", f=HD),
                                      T[BANK[k][name]][:, :, :].rearrange("p t (h f) -> p t h f", f=HD),
                                      V[k][:, :, :, 0:HD], ALU.subtract).then_inc(sem(f"t{k}_freed"), 1)
                elif name == "out":
                    n = {1: 0, 2: 2, 3: 3}[k]
                    wait(dve, *mm_done(k, name, seq))
                    wait(dve, sem(f"x_biased{n}"), seq.count(1, 1))
                    src, dst = {1: (X[0], X[1]), 2: (X[2], X[3]), 3: (X[4], X[4])}[k]
                    if k == 2:
                        wait(dve, sem("x_biased3"), seq.count(1, 0))
                    dve.tensor_tensor(dst[:, :, :], T[BANK[k][name]][:, :, :], src[:, :, :],
                                      ALU.add).then_inc(sem(f"t{k}_freed"), 1)
                elif name == "down3":
                    n = {1: 1, 3: 4}[k]
                    wait(dve, *mm_done(k, "down", seq))
                    wait(dve, sem(f"x_biased{n}"), seq.count(1, 1))
                    src, dst = {1: (X[1], X[2]), 3: (X[4], X[4])}[k]
                    if k == 1:
                        wait(dve, *freed(2, "out", seq + -1))
                    dve.tensor_tensor(dst[:, :, :], T[BANK[k]["down"]][:, :, :], src[:, :, :],
                                      ALU.add).then_inc(sem(f"t{k}_freed"), 1)
                elif name == "router":
                    dve.tensor_copy(router_w2, smalls[:, RW2:RW2 + 1].to_broadcast([P, P])).then_inc(
                        sem("w2_spread"), 1)
                    dve.wait_ge(sem("qk_low1"), 2)
                    for c in range(KC):
                        for n in range(NBLK):
                            ins = dve.tensor_reduce(kmean[:, c, n:n + 1],
                                                    parts[c][:, :, 1, n * BLOCK:(n + 1) * BLOCK],
                                                    axis=AX.XY, op=ALU.add)
                    ins.then_inc(sem("k_sums"), 1)
                    dve.wait_ge(sem("k_sums"), 1)
                    dve.tensor_scalar_mul(kmean[:, :, :], kmean[:, :, :], 1.0 / BLOCK).then_inc(sem("k_means"), 1)
                    dve.wait_ge(sem("router_score"), 1)
                    dve.tensor_scalar(keep[:, :], T[1][:, 1, 0:NBLK], smalls[:, RB2:RB2 + 1], 0.0, ALU.add,
                                      ALU.is_gt).then_inc(sem("keep_steps"), 1)
                    dve.wait_ge(sem("keep_steps"), 1)
                    dve.wait_ge(sem("causal_ready"), TT)
                    dve.tensor_copy(keep_k[:, 0, :].rearrange("p (n t) -> p n t", t=BLOCK),
                                    keep[:, :].unsqueeze(2).to_broadcast([P, NBLK, BLOCK]))
                    for t in range(TT):
                        for half in range(2):
                            at = slice(half * BLOCK, (half + 1) * BLOCK)
                            n = 2 * t + half
                            ins = dve.tensor_copy(keep_q[at, t:t + 1], keep[at, n:n + 1])
                    ins.then_inc(sem("keep_steps"), 1)
                    dve.wait_ge(sem("keep_steps"), 2)
                    for t in range(TT):
                        dve.tensor_scalar(rest[:, t, :], keep_k[:, 0, :], keep_q[:, t:t + 1], -BLOCKED, ALU.mult,
                                          ALU.mult).then_inc(sem("keep_steps"), 1)
                        dve.wait_ge(sem("keep_steps"), 3 + 2 * t)
                        dve.tensor_scalar_add(rest[:, t, :], rest[:, t, :], BLOCKED).then_inc(sem("keep_steps"), 1)
                        dve.wait_ge(sem("keep_steps"), 4 + 2 * t)
                        dve.tensor_tensor(mask_add[1][:, t, :], mask_add[1][:, t, :], rest[:, t, :],
                                          ALU.max).then_inc(sem("sparse_ready"), 1)

            stream(dve, dve.Fori, [sums, minimum, low_half, outputs, PIECES], piece)

        @block.tensor
        def _(pe):
            pe.wait_ge(sem("small_loaded"), 16)
            for n, u in enumerate(units):
                if u in NORM_OF:
                    pe.wait_ge(sem(f"w_loaded{n % STAGES}"), 16 * (n // STAGES + 1))
                    m = normed.index(u)
                    if m >= 2:
                        pe.wait_ge(sem("bias_col"), 1 + biased.index(normed[m - 2]))
                    s0 = SHIFT0 + 2 * NORM_OF[u]
                    for oc in range(KC):
                        for kc in range(KC):
                            ins = pe.matmul(T[bias_banks[m % 2]][:, 0, BCOL[u] + oc:BCOL[u] + oc + 1],
                                            stage[:, n % STAGES, kc, oc * P:(oc + 1) * P], smalls[:, s0 + kc:s0 + kc + 1],
                                            start=(kc == 0), stop=(kc == KC - 1))
                    ins.then_inc(sem("bias_product"), 1)
                if u[0] == "o":
                    pe.wait_ge(sem(f"w_loaded{n % STAGES}"), 16 * (n // STAGES + 1))
                    pe.wait_ge(sem("bv_spread"), int(u[1]) + 1)
                    if int(u[1]):
                        pe.wait_ge(sem("row_ready"), int(u[1]))
                    for kc in range(KC):
                        ins = pe.matmul(T[1][:, 0, :], bvb[:, kc, 0:P], stage[:, n % STAGES, kc, :],
                                        start=(kc == 0), stop=(kc == KC - 1))
                    ins.then_inc(sem("row_product"), 1)
            pe.wait_ge(sem("start_done"), 1)
            pe.wait_ge(sem("ident_ready"), 1)
            pe.wait_ge(sem("ones_set"), 3)

            def three(out, stat, move, first, last, lone=True):
                (sh, sl), (mh, ml) = stat, move
                pe.matmul(out, sh, mh, start=first, stop=False, skip_group_check=not lone)
                pe.matmul(out, sh, ml, start=False, stop=False, skip_group_check=not lone)
                return pe.matmul(out, sl, mh, start=False, stop=last, skip_group_check=not lone)

            def features(out, unit, oc, xh, xl):
                for kc in range(KC):
                    ins = three(out, (w_in(WH, unit, kc, oc * P, P), w_in(WL, unit, kc, oc * P, P)),
                                (xh[:, kc, :], xl[:, kc, :]), kc == 0, kc == KC - 1)
                return ins

            def tokens(out, t, unit, xh, xl, start=True, stop=True, lone=True):
                at = slice(t * P, (t + 1) * P)
                for kc in range(KC):
                    ins = three(out, (xh[:, kc, at], xl[:, kc, at]), (w_in(WH, unit, kc), w_in(WL, unit, kc)),
                                start and kc == 0, stop and kc == KC - 1, lone)
                return ins

            def scores(cur, prev, s):
                at = head(cur, prev, s, 0)
                if at:
                    a, seq, h = at
                    c, h8, r = h // HH, h % HH, RING[(a, h // HH)]
                    if h8 == 0:
                        wait(pe, sem(f"stack{a}_{c}"), seq.count(192, 192))
                    old = before(a, seq, h, 2)
                    if old:
                        wait(pe, sem(f"min_done{old[0]}"), old[1].count(H, old[2] + 1))
                    for qt in range(TT):
                        n = P if a == 1 and qt == 0 else S
                        ins = pe.matmul(SC[h % 2][:, qt, 0:n], QS[r][:, h8, qt * P:(qt + 1) * P],
                                        KS[r][:, h8, 0:n], start=True, stop=True)
                    ins.then_inc(sem(f"scores_done{a}"), 1)

            def turn(cur, prev, s):
                at = head(cur, prev, s, TURN_LAG)
                if at:
                    a, seq, h = at
                    wait(pe, sem(f"exp_done{a}"), seq.count(H, h + 1))
                    old = before(a, seq, h, 2)
                    if old:
                        wait(pe, sem(f"p_low{old[0]}"), old[1].count(H, old[2] + 1))
                    for qt in range(TT):
                        for kc in range(1 if a == 1 and qt == 0 else KC):
                            ins = pe.transpose(PT[h % 2][:, block_of(kc, qt), :], PR[:, place(a, h), qt, kc * P:(kc + 1) * P],
                                               ident[:, :])
                    ins.then_inc(sem(f"turned{a}"), 1)

            def products(cur, prev, s):
                at = head(cur, prev, s, AV_LAG)
                if at:
                    a, seq, h = at
                    if h == 0:
                        wait(pe, sem(f"v_low{a}"), seq.count(1, 1))
                    if h % GROUP == 0:
                        old = before(a, seq, h, 1)
                        if old:
                            wait(pe, sem(f"o_sum{old[0]}"), old[1].count(NG, old[2] // GROUP + 1))
                    wait(pe, sem(f"p_low{a}"), seq.count(H, h + 1))
                    for qt in range(TT):
                        nk = 1 if a == 1 and qt == 0 else KC
                        for kc in range(nk):
                            for half in (PH, PL):
                                ins = pe.matmul(AV[:, qt * GROUP + h % GROUP, :], half[place(a, h)][:, block_of(kc, qt), :], V[a][:, kc, h, :],
                                                start=(kc == 0 and half is PH), stop=(kc == nk - 1 and half is PL))
                    ins.then_inc(sem(f"av_done{a}"), 1)

            def turn_tile(src, bank, t):
                for kc in range(KC):
                    ins = pe.transpose(T[bank][:, kc, t * P:(t + 1) * P], src[:, t, kc * P:(kc + 1) * P], ident[:, :])
                return ins

            def piece(name, k, seq):
                for half in range(2):
                    half_piece(name, k, seq, half)

            def half_piece(name, k, seq, half):
                first, last = half == 0, half == 1
                if name.startswith("tr"):
                    src = {"trc": ctx_tok, "tro": o_tok}.get(name, xhat)
                    if first:
                        if name == "trc":
                            wait(pe, sem("ctx_loaded"), seq.count(16, 16))
                        elif name == "tro":
                            wait(pe, sem(f"o_ready{k - 1}"), seq.count(NG, NG))
                        else:
                            wait(pe, sem(f"ln{name[2]}_xhat"), seq.count(1, 1))
                        bank_free(pe, k, name, seq)
                    ins = turn_tile(src, BANK[k][name], half)
                    if last:
                        ins.then_inc(sem(f"t{k}_product"), 1)
                elif name in ("qk0", "qk1"):
                    c = int(name[2])
                    if first:
                        bank_free(pe, k, name, seq)
                        wait(pe, *freed(k, TRS[k][-1], seq))
                    xs = XH[acts(k, name)], XL[acts(k, name)]
                    if first:
                        features(T[BANK[k][name]][:, 0, :], f"q{k}", c, *xs)
                    else:
                        kx = (CH[1], CL[1]) if k == 2 else xs
                        features(T[BANK[k][name]][:, 1, :], f"k{k}", c, *kx).then_inc(sem(f"t{k}_product"), 1)
                elif name == "v":
                    if first:
                        bank_free(pe, k, name, seq)
                        if k == 2:
                            wait(pe, sem("ctx_carried"), seq.count(1, 1))
                    kx = (CH[1], CL[1]) if k == 2 else (XH[acts(k, name)], XL[acts(k, name)])
                    ins = tokens(T[BANK[k][name]][:, half, :], half, f"v{k}", *kx)
                    if last:
                        ins.then_inc(sem(f"t{k}_product"), 1)
                elif name == "outg":
                    if first:
                        bank_free(pe, k, "out", seq)
                        wait(pe, *freed(k, "trc", seq))
                    tokens(T[BANK[k]["out"]][:, half, :], half, "g0", CH[0], CL[0], start=first, stop=False,
                           lone=False)
                elif name == "out":
                    if first:
                        if k != 1:
                            bank_free(pe, k, name, seq)
                        wait(pe, *freed(k, "tro", seq))
                    ins = tokens(T[BANK[k][name]][:, half, :], half, f"o{k - 1}", XH[acts(k, name)], XL[acts(k, name)],
                                 start=k != 1, stop=True, lone=k != 1)
                    if last:
                        ins.then_inc(sem(f"t{k}_product"), 1)
                elif name in ("up0", "up1", "up2", "up3"):
                    if first:
                        bank_free(pe, k, name, seq)
                        if name == "up0":
                            wait(pe, *freed(k, "tr1" if k == 1 else "tr4", seq))
                    ins = features(T[BANK[k][name]][:, half, :], f"up{FFN_LAYER[k]}_{name[2]}", half, XH[acts(k, name)],
                                   XL[acts(k, name)])
                    if last:
                        ins.then_inc(sem(f"t{k}_product"), 1)
                elif name.startswith("down"):
                    q = int(name[4])
                    if first:
                        if q == 0:
                            bank_free(pe, k, "down", seq)
                        wait(pe, sem(f"h_low{k}"), seq.count(NQ, q + 1))
                    ins = tokens(T[BANK[k]["down"]][:, half, :], half, f"down{FFN_LAYER[k]}_{q}", hh[q % 2], hl[q % 2],
                                 start=q == 0 and first, stop=q == NQ - 1, lone=False)
                    if last and q < 2:
                        ins.then_inc(sem(f"down_part{k}"), 1)
                    elif last and q == NQ - 1:
                        ins.then_inc(sem(f"t{k}_product"), 1)
                elif name == "router" and first:
                    pe.wait_ge(sem("rw1_loaded"), 16)
                    pe.wait_ge(sem("k_means"), 1)
                    wait(pe, *freed(1, "v", Seq(None, 0)))
                    for c in range(KC):
                        ins = pe.matmul(T[1][:, 0, 0:NBLK], router_w1[:, c, :], kmean[:, c, :], start=(c == 0),
                                        stop=(c == KC - 1))
                    ins.then_inc(sem("router_hidden"), 1)
                    pe.wait_ge(sem("router_relu"), 1)
                    pe.wait_ge(sem("w2_spread"), 1)
                    pe.matmul(T[1][:, 1, 0:NBLK], router_w2, rhid[:, :], start=True,
                              stop=True).then_inc(sem("router_score"), 1)
                    pe.wait_ge(sem("keep_steps"), 1)

            stream(pe, pe.Fori, [scores, PIECES, turn, products], piece)


def kernel(**inputs):
    import numpy as _np
    import concourse.bacc as _bacc
    from concourse import mybir as _mybir
    from concourse.bass_utils import run_bass_kernel_spmd as _run

    def l0(n):
        return _np.asarray(inputs["L0_xattn_" + n])

    def l1(n):
        return _np.asarray(inputs["L1_xattn_" + n])

    def by_feature(w):
        return w.reshape(KC, HH, HD, -1).transpose(0, 2, 1, 3).reshape(D, -1)

    def unit(w):
        return w.T.reshape(KC, P, D).transpose(1, 0, 2).reshape(P, UNIT)

    def cols(v):
        return v.reshape(-1, P).T

    zero = _np.zeros(D, _np.float32)
    qkv, ca, cab = l1("qkv_w"), l1("ca_in_w"), l1("ca_in_b")
    w = {"q0": by_feature(l0("Wq")), "k0": by_feature(l0("Wk")), "v0": l0("Wv"), "o0": l0("Wo"), "g0": l0("Wg"),
         "q1": by_feature(qkv[0:D]), "k1": by_feature(qkv[D:2 * D]), "v1": qkv[2 * D:], "o1": l1("sa_out_w"),
         "q2": by_feature(ca[0:D]), "k2": by_feature(ca[D:2 * D]), "v2": ca[2 * D:], "o2": l1("ca_out_w")}
    b = {"q0": by_feature(l0("bq")), "k0": by_feature(l0("bk")), "v0": l0("bv"), "q1": zero, "k1": zero, "v1": zero,
         "q2": by_feature(cab[0:D]), "k2": by_feature(cab[D:2 * D]), "v2": cab[2 * D:]}
    for layer, (w1, b1, w2) in enumerate([(l0("W1"), l0("b1"), l0("W2")), (l1("ff_w1"), l1("ff_b1"), l1("ff_w2"))]):
        for q in range(NQ):
            at = slice(q * D, (q + 1) * D)
            w[f"up{layer}_{q}"], b[f"up{layer}_{q}"] = w1[at], b1[at]
            w[f"down{layer}_{q}"] = w2[:, at]
    norms = [(l0("g1"), l0("be1")), (l0("g2"), l0("be2")), (l1("n1_g"), l1("n1_b")), (l1("n2_g"), l1("n2_b")),
             (l1("n3_g"), l1("n3_b"))]
    small = _np.concatenate([cols(b[n]) for n in BIASED] + [cols(g) for g, _ in norms] + [cols(s) for _, s in norms]
                            + [cols(l1("r_b1")), cols(l1("r_w2")), _np.broadcast_to(l1("r_b2"), (P, 1))], axis=1)
    rows = _np.stack([l0("bo"), l0("b2"), l1("sa_out_b"), l1("ca_out_b"), l1("ff_b2"), l0("bg")])
    rw1 = by_feature(l1("r_w1").T).reshape(KC, P, P).transpose(1, 0, 2)
    arrays = {
        "x": inputs["x"], "ctx_in": inputs["ctx_1024"], "mask": inputs["mask_BxSxS2_fk0"],
        "weights": _np.stack([unit(w[n]) for n in UNITS]), "small": small,
        "rows": _np.broadcast_to(rows, (P, 6, D)), "rw1": rw1,
    }
    arrays = {n: _np.ascontiguousarray(a) for n, a in arrays.items()}
    nc = _bacc.Bacc("TRN2", target_bir_lowering=False, num_devices=1, dynamic_dma_scratch_size=1024)
    args = [nc.dram_tensor(n, a.shape, _mybir.dt.from_np(a.dtype), kind="ExternalInput").ap()
            for n, a in arrays.items()]
    out = nc.dram_tensor("out", (B, S, D), _mybir.dt.float32, kind="ExternalOutput").ap()
    program(nc, *args, out)
    r = _run(nc, [arrays], core_ids=[0])
    return r.results[0]["out"]
```
